# Optimizing a Trainium2 kernel written in Bass

```python
import numpy as np
import jax
import jax.numpy as jnp

def _softmax(x, axis=-1):
    return jax.nn.softmax(x, axis=axis)

def _gelu(x):
    return jax.nn.gelu(x, approximate=True)

def _silu(x):
    return jax.nn.silu(x)

def _sigmoid(x):
    return jax.nn.sigmoid(x)

def _layernorm(x, axis=-1, eps=1e-05):
    m = jnp.mean(x, axis=axis, keepdims=True)
    v = jnp.var(x, axis=axis, keepdims=True)
    return (x - m) / jnp.sqrt(v + eps)

def _scatter_add(tgt, idx, src, axis=0):
    return tgt.at[idx].add(src)

def _segment_sum(src, seg, n):
    return jax.ops.segment_sum(src, seg, n)
kernel_name = 'mk_gps_d2_gnn_r8_09fae6'

def setup_inputs(seed: int=0):
    np.random.seed(seed)
    _w = jnp.asarray

    def _rec_inputs():
        import jax
        import jax.numpy as jnp
        _gk = jax.random.key(seed)
        x = -0.0002117 + 1 * jax.random.normal(jax.random.fold_in(_gk, 1), (6250, 256), jnp.float32)
        src = jax.random.randint(jax.random.fold_in(_gk, 2), (100000,), 0, 6250, jnp.int32)
        dst = jnp.minimum((6250 * jax.random.uniform(jax.random.fold_in(_gk, 3), (100000,)) ** 2.0).astype(jnp.int32), 49999)
        _o = jnp.argsort(dst, stable=True)
        src = src[_o]
        dst = dst[_o]
        edge_attr_2 = jax.random.uniform(jax.random.fold_in(_gk, 12), (100000, 2), jnp.float32, 0.0, 1)
        return (x, src, dst, edge_attr_2)
    x, src, dst, edge_attr_2 = _rec_inputs()

    def _L0_gnn_setup():
        import jax, jax.numpy as jnp
        import numpy as np
        N_NODES = 12500
        N_EDGES = 200000
        IN_FEATS = 256
        OUT_FEATS = 64
        NUM_HEADS = 4
        key = jax.random.key(seed)
        k_h, k_adj, k_dir, k_wf, k_wr, k_af = jax.random.split(key, 6)
        h = jax.random.normal(k_h, (N_NODES, IN_FEATS), dtype=jnp.float32)
        adj = jax.random.randint(k_adj, (2, N_EDGES), 0, N_NODES, dtype=jnp.int64)
        bit = jax.random.randint(k_dir, (N_EDGES,), 0, 2).astype(jnp.float32)
        direction = jnp.stack([bit, 1.0 - bit], axis=1)
        s_w = float(np.sqrt(6.0 / (IN_FEATS + OUT_FEATS)))
        s_a = float(np.sqrt(6.0 / (NUM_HEADS + OUT_FEATS)))
        W_forward = jax.random.uniform(k_wf, (OUT_FEATS, IN_FEATS), jnp.float32, -s_w, s_w)
        W_reverse = jax.random.uniform(k_wr, (OUT_FEATS, IN_FEATS), jnp.float32, -s_w, s_w)
        attn_forward = jax.random.uniform(k_af, (1, NUM_HEADS, OUT_FEATS), jnp.float32, -s_a, s_a)
        return {'h': h, 'adj': adj, 'direction': direction, 'W_forward': W_forward, 'W_reverse': W_reverse, 'attn_forward': attn_forward}
    _L0_gnn_all = _L0_gnn_setup()
    _L0_gnn_in = {k: v for k, v in _L0_gnn_all.items() if k in ('W_forward', 'W_reverse', 'attn_forward')}
    del _L0_gnn_all

    def _L0_mix_setup():
        import jax, jax.numpy as jnp
        import numpy as np
        B, L, D, H = (4, 2048, 256, 8)
        DK = D // H

        def _heads(t):
            b, l, d = t.shape
            return t.reshape(b, l, H, DK).transpose(0, 2, 1, 3)
        key = jax.random.key(seed)
        ks = jax.random.split(key, 9)
        s = 0.02
        return {'x': jax.random.normal(ks[0], (B, L, D), dtype=jnp.float32), 'Wq': jax.random.normal(ks[1], (D, D), dtype=jnp.float32) * s, 'bq': jnp.zeros((D,), dtype=jnp.float32), 'Wk': jax.random.normal(ks[2], (D, D), dtype=jnp.float32) * s, 'bk': jnp.zeros((D,), dtype=jnp.float32), 'Wv': jax.random.normal(ks[3], (D, D), dtype=jnp.float32) * s, 'bv': jnp.zeros((D,), dtype=jnp.float32), 'Wfc': jax.random.normal(ks[4], (D, D), dtype=jnp.float32) * s, 'bfc': jnp.zeros((D,), dtype=jnp.float32)}
    _L0_mix_all = _L0_mix_setup()
    _L0_mix_in = {k: v for k, v in _L0_mix_all.items() if k in ('Wq', 'bq', 'Wk', 'bk', 'Wv', 'bv', 'Wfc', 'bfc')}
    del _L0_mix_all

    def _L0_ffn_setup():
        import jax, jax.numpy as jnp
        import numpy as np
        DIM = 256
        H = 8
        D = 64
        G = 64
        INNER = H * D
        SCALE = D ** (-0.5)
        key = jax.random.key(seed)
        ks = jax.random.split(key, 12)
        B, N = (4, 2048)
        x = jax.random.normal(ks[0], (B, N, DIM), dtype=jnp.float32)
        s = lambda fan_in: 1.0 / np.sqrt(fan_in)
        W_fx = jax.random.normal(ks[1], (DIM, INNER), dtype=jnp.float32) * s(DIM)
        b_fx = jnp.zeros((INNER,), dtype=jnp.float32)
        W_x = jax.random.normal(ks[2], (DIM, INNER), dtype=jnp.float32) * s(DIM)
        b_x = jnp.zeros((INNER,), dtype=jnp.float32)
        A = jax.random.normal(ks[3], (G, D), dtype=jnp.float32)
        Q, _ = jnp.linalg.qr(A.T)
        W_slice = Q[:, :G].astype(jnp.float32)
        b_slice = jnp.zeros((G,), dtype=jnp.float32)
        W_q = jax.random.normal(ks[4], (D, D), dtype=jnp.float32) * s(D)
        W_k = jax.random.normal(ks[5], (D, D), dtype=jnp.float32) * s(D)
        W_v = jax.random.normal(ks[6], (D, D), dtype=jnp.float32) * s(D)
        W_out = jax.random.normal(ks[7], (INNER, DIM), dtype=jnp.float32) * s(INNER)
        b_out = jnp.zeros((DIM,), dtype=jnp.float32)
        temperature = jnp.ones((1, H, 1, 1), dtype=jnp.float32) * 0.5
        return {'x': x, 'W_fx': W_fx, 'b_fx': b_fx, 'W_x': W_x, 'b_x': b_x, 'W_slice': W_slice, 'b_slice': b_slice, 'W_q': W_q, 'W_k': W_k, 'W_v': W_v, 'W_out': W_out, 'b_out': b_out, 'temperature': temperature}
    _L0_ffn_all = _L0_ffn_setup()
    _L0_ffn_in = {k: v for k, v in _L0_ffn_all.items() if k in ('W_fx', 'b_fx', 'W_x', 'b_x', 'W_slice', 'b_slice', 'W_q', 'W_k', 'W_v', 'W_out', 'b_out', 'temperature')}
    del _L0_ffn_all

    def _L1_gnn_setup():
        import jax, jax.numpy as jnp
        import numpy as np
        N = 2500
        E = 40000
        HID = 256
        HEADS = 8
        HD = HID // HEADS
        key = jax.random.key(seed)
        ks = jax.random.split(key, 12)
        scale = 1.0 / np.sqrt(HID).astype(np.float32)

        def lin_w(k):
            return jax.random.normal(k, (HID, HID), jnp.float32) * scale

        def lin_b(k):
            return jax.random.normal(k, (HID,), jnp.float32) * 0.01
        return {'h': jax.random.normal(ks[0], (N, HID), jnp.float32), 'Wq': lin_w(ks[1]), 'bq': lin_b(ks[2]), 'Wk': lin_w(ks[3]), 'bk': lin_b(ks[4]), 'Wv': lin_w(ks[5]), 'bv': lin_b(ks[6]), 'Wo': lin_w(ks[7]), 'bo': lin_b(ks[8]), 'rows': jax.random.randint(ks[9], (E,), 0, N), 'cols': jax.random.randint(ks[10], (E,), 0, N)}
    _L1_gnn_all = _L1_gnn_setup()
    _L1_gnn_in = {k: v for k, v in _L1_gnn_all.items() if k in ('Wq', 'bq', 'Wk', 'bk', 'Wv', 'bv', 'Wo', 'bo')}
    del _L1_gnn_all

    def _L1_mix_setup():
        import jax, jax.numpy as jnp
        import numpy as np
        D_MODEL = 256
        NUM_HEADS = 8
        DEPTH = D_MODEL // NUM_HEADS
        B, L = (32, 512)

        def _feature_map(x):
            return jax.nn.elu(x) + 1.0
        key = jax.random.key(seed)
        ks = jax.random.split(key, 9)
        sc = 1.0 / np.sqrt(D_MODEL)
        return {'x': jax.random.normal(ks[0], (B, L, D_MODEL), dtype=jnp.float32), 'wq': jax.random.normal(ks[1], (D_MODEL, D_MODEL), dtype=jnp.float32) * sc, 'bq': jnp.zeros((D_MODEL,), dtype=jnp.float32), 'wk': jax.random.normal(ks[2], (D_MODEL, D_MODEL), dtype=jnp.float32) * sc, 'bk': jnp.zeros((D_MODEL,), dtype=jnp.float32), 'wv': jax.random.normal(ks[3], (D_MODEL, D_MODEL), dtype=jnp.float32) * sc, 'bv': jnp.zeros((D_MODEL,), dtype=jnp.float32), 'wo': jax.random.normal(ks[4], (D_MODEL, D_MODEL), dtype=jnp.float32) * sc, 'bo': jnp.zeros((D_MODEL,), dtype=jnp.float32)}
    _L1_mix_all = _L1_mix_setup()
    _L1_mix_in = {k: v for k, v in _L1_mix_all.items() if k in ('wq', 'bq', 'wk', 'bk', 'wv', 'bv', 'wo', 'bo')}
    del _L1_mix_all

    def _L1_ffn_setup():
        import jax, jax.numpy as jnp
        import numpy as np
        N_EXPERTS = 8
        TOP_K = 2
        key = jax.random.key(seed)
        ks = jax.random.split(key, 5)
        B, T, C, E, H = (8, 256, 256, 8, 682)
        scale = 1.0 / np.sqrt(C)
        return {'x': jax.random.normal(ks[0], (B, T, C), dtype=jnp.float32), 'router_w': jax.random.normal(ks[1], (E, C), dtype=jnp.float32) * scale, 'w1': jax.random.normal(ks[2], (E, H, C), dtype=jnp.float32) * scale, 'w2': jax.random.normal(ks[3], (E, C, H), dtype=jnp.float32) * (1.0 / np.sqrt(H)), 'w3': jax.random.normal(ks[4], (E, H, C), dtype=jnp.float32) * scale}
    _L1_ffn_all = _L1_ffn_setup()
    _L1_ffn_in = {k: v for k, v in _L1_ffn_all.items() if k in ('router_w', 'w1', 'w2', 'w3')}
    del _L1_ffn_all
    return {'x': x, 'src': src, 'dst': dst, 'edge_attr_2': edge_attr_2, 'L0_gnn_W_forward': _L0_gnn_in['W_forward'], 'L0_gnn_W_reverse': _L0_gnn_in['W_reverse'], 'L0_gnn_attn_forward': _L0_gnn_in['attn_forward'], 'L0_mix_Wq': _L0_mix_in['Wq'], 'L0_mix_bq': _L0_mix_in['bq'], 'L0_mix_Wk': _L0_mix_in['Wk'], 'L0_mix_bk': _L0_mix_in['bk'], 'L0_mix_Wv': _L0_mix_in['Wv'], 'L0_mix_bv': _L0_mix_in['bv'], 'L0_mix_Wfc': _L0_mix_in['Wfc'], 'L0_mix_bfc': _L0_mix_in['bfc'], 'L0_ffn_W_fx': _L0_ffn_in['W_fx'], 'L0_ffn_b_fx': _L0_ffn_in['b_fx'], 'L0_ffn_W_x': _L0_ffn_in['W_x'], 'L0_ffn_b_x': _L0_ffn_in['b_x'], 'L0_ffn_W_slice': _L0_ffn_in['W_slice'], 'L0_ffn_b_slice': _L0_ffn_in['b_slice'], 'L0_ffn_W_q': _L0_ffn_in['W_q'], 'L0_ffn_W_k': _L0_ffn_in['W_k'], 'L0_ffn_W_v': _L0_ffn_in['W_v'], 'L0_ffn_W_out': _L0_ffn_in['W_out'], 'L0_ffn_b_out': _L0_ffn_in['b_out'], 'L0_ffn_temperature': _L0_ffn_in['temperature'], 'L1_gnn_Wq': _L1_gnn_in['Wq'], 'L1_gnn_bq': _L1_gnn_in['bq'], 'L1_gnn_Wk': _L1_gnn_in['Wk'], 'L1_gnn_bk': _L1_gnn_in['bk'], 'L1_gnn_Wv': _L1_gnn_in['Wv'], 'L1_gnn_bv': _L1_gnn_in['bv'], 'L1_gnn_Wo': _L1_gnn_in['Wo'], 'L1_gnn_bo': _L1_gnn_in['bo'], 'L1_mix_wq': _L1_mix_in['wq'], 'L1_mix_bq': _L1_mix_in['bq'], 'L1_mix_wk': _L1_mix_in['wk'], 'L1_mix_bk': _L1_mix_in['bk'], 'L1_mix_wv': _L1_mix_in['wv'], 'L1_mix_bv': _L1_mix_in['bv'], 'L1_mix_wo': _L1_mix_in['wo'], 'L1_mix_bo': _L1_mix_in['bo'], 'L1_ffn_router_w': _L1_ffn_in['router_w'], 'L1_ffn_w1': _L1_ffn_in['w1'], 'L1_ffn_w2': _L1_ffn_in['w2'], 'L1_ffn_w3': _L1_ffn_in['w3']}

def reference(x, src, dst, edge_attr_2, L0_gnn_W_forward, L0_gnn_W_reverse, L0_gnn_attn_forward, L0_mix_Wq, L0_mix_bq, L0_mix_Wk, L0_mix_bk, L0_mix_Wv, L0_mix_bv, L0_mix_Wfc, L0_mix_bfc, L0_ffn_W_fx, L0_ffn_b_fx, L0_ffn_W_x, L0_ffn_b_x, L0_ffn_W_slice, L0_ffn_b_slice, L0_ffn_W_q, L0_ffn_W_k, L0_ffn_W_v, L0_ffn_W_out, L0_ffn_b_out, L0_ffn_temperature, L1_gnn_Wq, L1_gnn_bq, L1_gnn_Wk, L1_gnn_bk, L1_gnn_Wv, L1_gnn_bv, L1_gnn_Wo, L1_gnn_bo, L1_mix_wq, L1_mix_bq, L1_mix_wk, L1_mix_bk, L1_mix_wv, L1_mix_bv, L1_mix_wo, L1_mix_bo, L1_ffn_router_w, L1_ffn_w1, L1_ffn_w2, L1_ffn_w3):
    import jax
    import jax.numpy as jnp

    def _L0_gnn_ref(h, adj, direction, W_forward, W_reverse, attn_forward):
        import jax, jax.numpy as jnp
        import numpy as np
        N_NODES = 12500
        N_EDGES = 200000
        IN_FEATS = 256
        OUT_FEATS = 64
        NUM_HEADS = 4
        N = h.shape[0]
        H = attn_forward.shape[1]
        h_fwd = h @ W_forward.T
        h_rev = h @ W_reverse.T
        src, dst = (adj[0], adj[1])
        messages = h_fwd[src] * direction[:, 0:1] + h_rev[src] * direction[:, 1:2]
        scores = jnp.einsum('ef,hf->eh', messages, attn_forward[0])
        scores = jax.nn.leaky_relu(scores, negative_slope=0.2)
        exp_scores = jnp.exp(scores - scores.max(axis=0, keepdims=True))
        sum_exp = jax.ops.segment_sum(exp_scores, dst, num_segments=N)
        norm = exp_scores / (sum_exp[dst] + 1e-10)
        outs = [jax.ops.segment_sum(messages * norm[:, hd:hd + 1], dst, num_segments=N) for hd in range(H)]
        out = jnp.stack(outs, axis=1)
        return out.reshape(N, -1)

    def _L0_mix_ref(x, Wq, bq, Wk, bk, Wv, bv, Wfc, bfc):
        import jax, jax.numpy as jnp
        import numpy as np
        B, L, D, H = (4, 2048, 256, 8)
        DK = D // H

        def _heads(t):
            b, l, d = t.shape
            return t.reshape(b, l, H, DK).transpose(0, 2, 1, 3)
        q = _heads(x @ Wq.T + bq)
        k = _heads(x @ Wk.T + bk)
        v = _heads(x @ Wv.T + bv)
        seq_len = q.shape[-2]
        p_attn = jnp.einsum('bhnd,bhne->bhde', k, v) / seq_len
        out = jnp.einsum('bhnd,bhde->bhne', q, p_attn)
        out = out.transpose(0, 2, 1, 3).reshape(x.shape[0], seq_len, H * DK)
        return out @ Wfc.T + bfc

    def _L0_ffn_ref(x, W_fx, b_fx, W_x, b_x, W_slice, b_slice, W_q, W_k, W_v, W_out, b_out, temperature):
        import jax, jax.numpy as jnp
        import numpy as np
        DIM = 256
        H = 8
        D = 64
        G = 64
        INNER = H * D
        SCALE = D ** (-0.5)
        B, N, _ = x.shape
        fx_mid = (x @ W_fx + b_fx).reshape(B, N, H, D).transpose(0, 2, 1, 3)
        x_mid = (x @ W_x + b_x).reshape(B, N, H, D).transpose(0, 2, 1, 3)
        temp = jnp.clip(temperature, 0.1, 5.0)
        slice_weights = jax.nn.softmax((x_mid @ W_slice + b_slice) / temp, axis=-1)
        slice_norm = slice_weights.sum(axis=2)
        slice_token = jnp.einsum('bhnc,bhng->bhgc', fx_mid, slice_weights)
        slice_token = slice_token / (slice_norm[..., None] + 1e-05)
        q = slice_token @ W_q
        k = slice_token @ W_k
        v = slice_token @ W_v
        attn = jax.nn.softmax(jnp.einsum('bhgc,bhkc->bhgk', q, k) * SCALE, axis=-1)
        out_slice = jnp.einsum('bhgk,bhkc->bhgc', attn, v)
        out_x = jnp.einsum('bhgc,bhng->bhnc', out_slice, slice_weights)
        out_x = out_x.transpose(0, 2, 1, 3).reshape(B, N, INNER)
        return out_x @ W_out + b_out

    def _L1_gnn_ref(h, Wq, bq, Wk, bk, Wv, bv, Wo, bo, rows, cols):
        import jax, jax.numpy as jnp
        import numpy as np
        N = 2500
        E = 40000
        HID = 256
        HEADS = 8
        HD = HID // HEADS
        n = h.shape[0]
        scaling = HD ** (-0.5)
        q = (h @ Wq + bq).reshape(n, HD, HEADS) * scaling
        k = (h @ Wk + bk).reshape(n, HD, HEADS)
        v = (h @ Wv + bv).reshape(n, HD, HEADS)
        s = jnp.einsum('edh,edh->eh', q[rows], k[cols])
        m = jax.ops.segment_max(s, rows, num_segments=n)
        e = jnp.exp(s - m[rows])
        z = jax.ops.segment_sum(e, rows, num_segments=n)
        attn = e / z[rows]
        out = jax.ops.segment_sum(attn[:, None, :] * v[cols], rows, num_segments=n)
        return out.reshape(n, -1) @ Wo + bo

    def _L1_mix_ref(x, wq, bq, wk, bk, wv, bv, wo, bo):
        import jax, jax.numpy as jnp
        import numpy as np
        D_MODEL = 256
        NUM_HEADS = 8
        DEPTH = D_MODEL // NUM_HEADS
        B, L = (32, 512)

        def _feature_map(x):
            return jax.nn.elu(x) + 1.0
        b, l, _ = x.shape
        q = (x @ wq + bq).reshape(b, l, NUM_HEADS, DEPTH)
        k = (x @ wk + bk).reshape(b, l, NUM_HEADS, DEPTH)
        v = (x @ wv + bv).reshape(b, l, NUM_HEADS, DEPTH)
        q = _feature_map(q)
        k = _feature_map(k)
        kv = jnp.einsum('blhd,blhe->bhde', k, v)
        k_sum = jnp.sum(k, axis=1)
        qkv = jnp.einsum('blhd,bhde->blhe', q, kv)
        normalizer = jnp.einsum('blhd,bhd->blh', q, k_sum) + 1e-06
        out = qkv / normalizer[..., None]
        out = out.reshape(b, l, D_MODEL)
        return out @ wo + bo

    def _L1_ffn_ref(x, router_w, w1, w2, w3):
        import jax, jax.numpy as jnp
        import numpy as np
        N_EXPERTS = 8
        TOP_K = 2
        B, T, C = x.shape
        flat = x.reshape(-1, C)
        logits = flat @ router_w.T
        probs = jax.nn.softmax(logits, axis=-1)
        topk_probs, topk_idx = jax.lax.top_k(probs, TOP_K)
        topk_probs = topk_probs / (jnp.sum(topk_probs, axis=-1, keepdims=True) + 1e-09)
        onehot = jax.nn.one_hot(topk_idx, N_EXPERTS, dtype=flat.dtype)
        gates = jnp.einsum('nk,nke->ne', topk_probs, onehot)
        h1 = jnp.einsum('nc,ehc->neh', flat, w1)
        h3 = jnp.einsum('nc,ehc->neh', flat, w3)
        h = jax.nn.silu(h1) * h3
        y = jnp.einsum('neh,ech->nec', h, w2)
        out = jnp.einsum('ne,nec->nc', gates, y)
        return out.reshape(B, T, C)
    edge_index = jnp.stack([src, dst])
    xn = _layernorm(x, axis=-1)
    x = x + _L0_gnn_ref(xn, edge_index, edge_attr_2, L0_gnn_W_forward, L0_gnn_W_reverse, L0_gnn_attn_forward) + _L0_mix_ref(xn[None], L0_mix_Wq, L0_mix_bq, L0_mix_Wk, L0_mix_bk, L0_mix_Wv, L0_mix_bv, L0_mix_Wfc, L0_mix_bfc)[0]
    x = x + _L0_ffn_ref(_layernorm(x, axis=-1)[None], L0_ffn_W_fx, L0_ffn_b_fx, L0_ffn_W_x, L0_ffn_b_x, L0_ffn_W_slice, L0_ffn_b_slice, L0_ffn_W_q, L0_ffn_W_k, L0_ffn_W_v, L0_ffn_W_out, L0_ffn_b_out, L0_ffn_temperature)[0]
    xn = _layernorm(x, axis=-1)
    x = x + _L1_gnn_ref(xn, L1_gnn_Wq, L1_gnn_bq, L1_gnn_Wk, L1_gnn_bk, L1_gnn_Wv, L1_gnn_bv, L1_gnn_Wo, L1_gnn_bo, src, dst) + _L1_mix_ref(xn[None], L1_mix_wq, L1_mix_bq, L1_mix_wk, L1_mix_bk, L1_mix_wv, L1_mix_bv, L1_mix_wo, L1_mix_bo)[0]
    x = x + _L1_ffn_ref(_layernorm(x, axis=-1)[None], L1_ffn_router_w, L1_ffn_w1, L1_ffn_w2, L1_ffn_w3)[0]
    return x

_drawn_inputs = setup_inputs


def setup_inputs(seed=0):
    import zlib

    import numpy as np

    out = dict(_drawn_inputs(seed))
    spreads = {'L0_mix_bq': (0.0, 0.489),
     'L0_mix_bk': (0.0, 0.44),
     'L0_mix_bv': (0.0, 0.444),
     'L0_mix_bfc': (0.0, 0.1),
     'L0_ffn_b_fx': (0.0, 0.1),
     'L0_ffn_b_x': (0.0, 0.492),
     'L0_ffn_b_slice': (0.0, 0.651),
     'L0_ffn_b_out': (0.0, 0.1),
     'L0_ffn_temperature': (0.5, 0.6),
     'L1_mix_bq': (0.0, 2.0),
     'L1_mix_bk': (0.0, 2.0),
     'L1_mix_bv': (0.0, 0.1),
     'L1_mix_bo': (0.0, 0.1)}
    factors = {'L0_mix_Wq': 3.032,
     'L0_mix_Wk': 3.653,
     'L0_mix_Wv': 4.047,
     'L0_mix_Wfc': 3.188,
     'L0_ffn_W_slice': 3.244,
     'L0_ffn_W_q': 8.0,
     'L0_ffn_W_k': 8.0,
     'L1_gnn_bq': 19.172,
     'L1_gnn_bk': 64.0,
     'L1_gnn_bo': 2.686,
     'L1_mix_wq': 3.571,
     'L1_mix_wk': 2.758,
     'L1_gnn_bv': 3.979}
    for name, (base, spread) in spreads.items():
        noise = np.random.default_rng([zlib.crc32(name.encode()), seed]).standard_normal(out[name].shape)
        drawn = base * np.exp(spread * noise) if base else spread * noise
        out[name] = jnp.asarray(drawn.astype(out[name].dtype))
    for name, factor in factors.items():
        out[name] = (out[name] * factor).astype(out[name].dtype)
    return out
```

```python
from contextlib import ExitStack

import concourse.bass as bass
import numpy as np
from concourse import mybir

ALU = mybir.AluOpType
ACT = mybir.ActivationFunctionType
AX = mybir.AxisListType
F32 = mybir.dt.float32
BF16 = mybir.dt.bfloat16
I32 = mybir.dt.int32

P = 128
N, E, D = 6250, 100000, 256
NT = (N + P - 1) // P
NP = NT * P
LAST = N - (NT - 1) * P
BN = 32
NB = NP // BN + 1
PAD_KEY = NP
IN_TILES = 784
EP = IN_TILES * P
GROUP = 4
SORT_TILES = (EP + NB * (P - 1)) // P
SORT_TILES = (SORT_TILES + 4 * GROUP - 1) // (4 * GROUP) * (4 * GROUP)
REC = 4
FOUR = 4
ROW_MOVES = 40
BIG = 1.0e30
FLOOR = 1.0e20
EPS = 1e-5


class Phase(ExitStack):

    def __init__(self, nc):
        super().__init__()
        self.nc = nc
        self.semaphores = []

    def semaphore(self, name):
        self.semaphores.append(self.enter_context(self.nc.semaphore(name)))
        return self.semaphores[-1]

    def __exit__(self, *error):
        with self.nc.Block() as block:
            @block.gpsimd
            def _(pool):
                for s in self.semaphores:
                    pool.sem_clear(s)
        return super().__exit__(*error)


def row_moves(consts, count):
    return [consts["row_moves"].pop(0) for _ in range(count)]


def late(k, i, unroll, ring):
    return not isinstance(k, int) or unroll * k + i >= ring


def pipeline(eng, stages, count, unroll):
    most = max(0, *(lead for _, lead in stages))
    least = min(0, *(lead for _, lead in stages))
    first = -(-(unroll - least) // unroll)
    last = (count - most) // unroll

    def steps(k, places):
        for i in places:
            for stage, lead in stages:
                if isinstance(k, int) and not 0 <= unroll * k + i + lead < count:
                    continue
                stage(k + (i + lead) // unroll, (i + lead) % unroll)

    for k in range(-most // unroll, first):
        steps(k, range(unroll))
    with eng.Fori(first, last) as k:
        steps(k, range(unroll))
    for k in range(last, -(-(count - least) // unroll)):
        steps(k, range(unroll))


def register_values(nc, engine, ap, most):
    return nc.values_load_multi_w_load_instructions(
        ap, engines=(engine,), min_val=0, max_val=most,
        skip_runtime_bounds_check_because="the chip has made them within the bounds")[1]


def rows_of(ap, parts):
    return ap.unsqueeze(0).to_broadcast([parts, ap.shape[0]])


def sort_edges(nc, tag, key, other, attr, recs, tile_bucket, consts):
    RING = 8
    CHAINS = 4
    HALF = RING // 2
    AHEAD = 2
    with Phase(nc) as ctx:
        def sb(name, shape, dt):
            return ctx.enter_context(nc.sbuf_tensor(f"{tag}_{name}", shape, dt))

        def sem(name):
            return ctx.semaphore(f"{tag}_{name}")

        key_i = sb("key_i", [P, IN_TILES], I32)
        other_i = sb("other_i", [P, IN_TILES], I32)
        attr_f = sb("attr_f", [P, IN_TILES, 2], F32)
        rec = sb("rec", [P, IN_TILES, REC], F32)
        bucket_i = sb("bucket_i", [P, IN_TILES], I32)
        bucket_f = sb("bucket_f", [P, IN_TILES + RING], F32)
        empty = sb("empty", [P, SORT_TILES, REC], F32)
        onehot = sb("onehot", [P, RING, NB], BF16)
        scratch = sb("scratch", [P, 2, NB], F32)
        count_i = sb("count_i", [P, NB], I32)
        tiles_i = sb("tiles_i", [P, NB], I32)
        tiles_f = sb("tiles_f", [P, NB], F32)
        ends = sb("ends", [P, NB], F32)
        start = sb("start", [P, NB], F32)
        ones_row = sb("ones_row", [P, NB], F32)
        bmap = sb("bmap", [P, 8], F32)
        bmap_i = sb("bmap_i", [P, 8], I32)
        slot = sb("slot", [P, 2, 4], F32)
        slot_i = sb("slot_i", [P, 2, 4], I32)
        slot_t = sb("slot_t", [P, 2, 4], I32)
        slot_p = sb("slot_p", [P, 2, 4], I32)
        row = [sb(f"row{i}", [P, 4], I32) for i in range(2)]
        stage = [sb(f"stage{i}", [P, REC], F32) for i in range(RING)]
        counts = [ctx.enter_context(nc.psum_tensor(f"{tag}_counts{i}", [P, 512], F32)) for i in range(CHAINS)]
        total = ctx.enter_context(nc.psum_tensor(f"{tag}_total", [P, 512], F32))
        tri, comp, ones, ident, iota_b = (consts[k] for k in ("tri", "comp", "ones", "ident", "iota_b"))

        loaded = sem("loaded")
        split = sem("split")
        emptied = sem("emptied")
        hot = sem("hot")
        counted = sem("counted")
        small = sem("small")
        started = sem("started")
        hot2 = sem("hot2")
        ranked = sem("ranked")
        read = sem("read")
        rowed = sem("rowed")
        staged = sem("staged")
        taken = sem("taken")
        mapped = sem("mapped")
        put = row_moves(consts, RING)

        with nc.Block() as block:
            @block.sync
            def _(sp):
                sp.dma_start(key_i[:], key).then_inc(loaded, 16)
                sp.dma_start(other_i[:], other).then_inc(loaded, 16)
                if attr is not None:
                    sp.dma_start(attr_f[:], attr).then_inc(loaded, 16)
                sp.wait_ge(split, 5)
                sp.dma_start(recs.rearrange("(p t) r -> p (t r)", p=P),
                             empty[:].rearrange("p t r -> p (t r)")).then_inc(emptied, 16)
                sp.wait_ge(small, 18)
                with nc.allow_non_contiguous_dma(reason="1024 words"):
                    sp.dma_start(tile_bucket.rearrange("(c p) -> p c", p=P), bmap_i[:]).then_inc(mapped, 16)
                sp.wait_ge(mapped, 16)
                sp.wait_ge(emptied, 16)

            @block.gpsimd
            def _(pool):
                pool.wait_ge(emptied, 16)
                with pool.Fori(0, IN_TILES // RING) as k:
                    for i in range(RING):
                        if i % 4 == 0:
                            pool.wait_ge(rowed, (k * 2 + i // 4 + 1) * 4)
                        pool.wait_ge(staged, k * RING + i + 1)
                        pool.sem_inc(taken, 1)
                        pool.indirect_dma_start(
                            out=recs, out_offset=bass.IndirectOffsetOnAxis(ap=row[i // 4][:, i % 4:i % 4 + 1], axis=0),
                            in_=stage[i][:], in_offset=None).then_inc(put[i], 16)
                for i in range(RING):
                    pool.wait_ge(put[i], 16 * (IN_TILES // RING))

            @block.scalar
            def _(act):
                act.wait_ge(split, 4)

                def copy_records(k):
                    for i in range(RING):
                        if late(k, i, RING, RING):
                            act.wait_ge(put[i], k * 16)
                        act.activation(stage[i][:], rec[:, bass.ds(k * RING + i, 1), :].rearrange("p a r -> p (a r)"),
                                       ACT.Copy).then_inc(staged, 1)

                copy_records(0)
                with act.Fori(1, IN_TILES // RING) as k:
                    copy_records(k)

            @block.tensor
            def _(pe):
                def count(k, first=False, last=False):
                    for half in range(2):
                        pe.wait_ge(hot, 2 * k + half + 1)
                        for c in range(HALF):
                            mm = pe.matmul(total[:, 0:NB], ones[:], onehot[:, HALF * half + c, :],
                                           start=first and (half, c) == (0, 0), stop=last and (half, c) == (1, HALF - 1))
                        mm.then_inc(counted, 1)

                count(0, first=True)
                with pe.Fori(1, IN_TILES // RING - 1) as k:
                    count(k)
                count(IN_TILES // RING - 1, last=True)
                pe.wait_ge(small, 7)
                for j in range(CHAINS):
                    pe.matmul(counts[j][:, 0:NB], ident[:], start[:], start=True, stop=True).then_inc(started, 1)
                pe.wait_ge(started, CHAINS)
                with pe.Fori(0, IN_TILES // RING) as k:
                    for i in range(RING):
                        bank = counts[i % CHAINS][:, 0:NB]
                        pe.wait_ge(read, k * RING + i + 1)
                        for back in range(CHAINS, 0, -1):
                            pe.matmul(bank, (comp if back == CHAINS else ones)[:], onehot[:, (i - back) % RING, :],
                                      start=False, stop=False, skip_group_check=True)
                        pe.wait_ge(hot2, k * RING + i + 1)
                        pe.matmul(bank, tri[:], onehot[:, i, :], start=False, stop=True,
                                  skip_group_check=True).then_inc(ranked, 1)

            @block.vector
            def _(dve):
                dve.memset(empty[:], 0.0).then_inc(split, 1)
                dve.wait_ge(loaded, 48 if attr is not None else 32)
                dve.wait_ge(split, 1)
                dve.tensor_copy(rec[:, :, 0], key_i[:]).then_inc(split, 1)
                dve.tensor_copy(rec[:, :, 1], other_i[:]).then_inc(split, 1)
                if attr is not None:
                    dve.tensor_copy(rec[:, :, 2:4], attr_f[:]).then_inc(split, 1)
                else:
                    dve.memset(rec[:, :, 2:4], 0.0).then_inc(split, 1)
                dve.memset(empty[:, :, 0:1], -1.0).then_inc(split, 1)
                dve.memset(bucket_f[:, IN_TILES:], -1.0).then_inc(split, 1)
                dve.tensor_scalar(bucket_i[:], key_i[:], 5, None, ALU.arith_shift_right).then_inc(split, 1)
                dve.wait_ge(split, 7)
                dve.tensor_copy(bucket_f[:, 0:IN_TILES], bucket_i[:]).then_inc(split, 1)
                dve.wait_ge(split, 8)

                def one_hot(t, place):
                    return dve.tensor_scalar(onehot[:, place, :], iota_b[:, 0:NB], bucket_f[:, bass.ds(t, 1)], None,
                                             ALU.is_equal)

                def one_hots(k):
                    for half in range(2):
                        if late(k, HALF * half, RING, RING):
                            dve.wait_ge(counted, 2 * (k - 1) + half + 1)
                        dve.tensor_tensor(
                            onehot[:, HALF * half:HALF * (half + 1), :],
                            iota_b[:, 0:NB].unsqueeze(1).to_broadcast([P, HALF, NB]),
                            bucket_f[:, bass.ds(k * RING + HALF * half, HALF)].unsqueeze(2).to_broadcast([P, HALF, NB]),
                            ALU.is_equal).then_inc(hot, 1)

                one_hots(0)
                with dve.Fori(1, IN_TILES // RING) as k:
                    one_hots(k)
                dve.wait_ge(counted, 2 * (IN_TILES // RING))
                dve.memset(ones_row[:], 1.0).then_inc(small, 1)
                dve.tensor_scalar(count_i[:], total[:, 0:NB], float(P - 1), None, ALU.add).then_inc(small, 1)
                dve.wait_ge(small, 2)
                dve.tensor_scalar(tiles_i[:], count_i[:], 7, None, ALU.arith_shift_right).then_inc(small, 1)
                dve.wait_ge(small, 3)
                dve.tensor_copy(tiles_f[:], tiles_i[:]).then_inc(small, 1)
                dve.wait_ge(small, 4)
                dve.tensor_tensor_scan(ends[:], ones_row[:], tiles_f[:], 0.0, ALU.mult, ALU.add).then_inc(small, 1)
                dve.wait_ge(small, 5)
                dve.tensor_tensor(start[:], ends[:], tiles_f[:], ALU.subtract).then_inc(small, 1)
                dve.wait_ge(small, 6)
                dve.tensor_scalar(start[:], start[:], float(P), None, ALU.mult).then_inc(small, 1)
                for c in range(8):
                    if c >= 2:
                        dve.wait_ge(small, 7 + c - 1)
                    dve.tensor_scalar(scratch[:, c % 2, :], ends[:], consts["tile_no"][:, c:c + 1], None, ALU.is_le,
                                      ALU.add, accum_out=bmap[:, c:c + 1]).then_inc(small, 1)
                dve.wait_ge(small, 15)
                dve.tensor_scalar(bmap[:], bmap[:], float(NB - 1), None, ALU.min).then_inc(small, 1)
                dve.wait_ge(small, 16)
                dve.tensor_copy(bmap_i[:], bmap[:]).then_inc(small, 1)
                dve.memset(onehot[:, RING - CHAINS:RING, :], 0.0).then_inc(small, 1)
                dve.wait_ge(small, 18)
                dve.wait_ge(started, CHAINS)
                dve.sem_inc(read, CHAINS)
                for i in range(AHEAD):
                    one_hot(i, i).then_inc(hot2, 1)
                dve.sem_inc(ranked, CHAINS)

                def rank(k):
                    for i in range(RING):
                        t, g = k * RING + i, i // 4
                        dve.wait_ge(ranked, t + AHEAD - CHAINS + 1 + CHAINS)
                        one_hot(t + AHEAD, (i + AHEAD) % RING).then_inc(hot2, 1)
                        dve.wait_ge(ranked, t + 1 + CHAINS)
                        dve.wait_ge(read, t - 1 + CHAINS)
                        dve.tensor_tensor_reduce(scratch[:, i % 2, :], onehot[:, i, :], counts[i % CHAINS][:, 0:NB],
                                                 1.0, 0.0, ALU.mult, ALU.add, slot[:, g, i % 4:i % 4 + 1]).then_inc(read, 1)
                        if i % 4 == 3:
                            base = (k * 2 + g) * 4
                            dve.wait_ge(read, t + 1 + CHAINS)
                            if late(k, i, RING, 4):
                                dve.wait_ge(rowed, base)
                            dve.tensor_copy(slot_i[:, g, :], slot[:, g, :]).then_inc(rowed, 1)
                            dve.wait_ge(rowed, base + 1)
                            dve.tensor_scalar(slot_t[:, g, :], slot_i[:, g, :], 7, None,
                                              ALU.arith_shift_right).then_inc(rowed, 1)
                            dve.tensor_scalar(slot_p[:, g, :], slot_i[:, g, :], P - 1, None,
                                              ALU.bitwise_and).then_inc(rowed, 1)
                            dve.wait_ge(rowed, base + 3)
                            if late(k, i, RING, RING):
                                for c in range(4):
                                    dve.wait_ge(put[4 * g + c], k * 16)
                            dve.scalar_tensor_tensor(row[g][:], slot_p[:, g, :], float(SORT_TILES), slot_t[:, g, :],
                                                     ALU.mult, ALU.add).then_inc(rowed, 1)

                rank(0)
                with dve.Fori(1, IN_TILES // RING) as k:
                    rank(k)


def make_constants(nc, ctx):
    def sb(name, shape, dt):
        return ctx.enter_context(nc.sbuf_tensor(name, shape, dt))

    c = {
        "ident": sb("ident", [P, P], F32),
        "ident_far": sb("ident_far", [P, P], BF16),
        "tri": sb("tri", [P, P], BF16),
        "comp": sb("comp", [P, P], BF16),
        "ones": sb("ones", [P, P], BF16),
        "iota_b": sb("iota_b", [P, NB], BF16),
        "node_no": sb("node_no", [P, 4, BN], BF16),
        "tile_no": sb("tile_no", [P, 8], F32),
        "head_rows": sb("head_rows", [P, 4], F32),
    }
    c["row_moves"] = [ctx.enter_context(nc.semaphore(f"row_moves{i}")) for i in range(ROW_MOVES)]
    zero = sb("const_zero", [P, P], F32)
    one = sb("const_one", [P, P], F32)
    made = ctx.enter_context(nc.semaphore("const_made"))
    with nc.Block() as block:
        @block.gpsimd
        def _(pool):
            pool.memset(zero[:], 0.0).then_inc(made, 1)
            pool.memset(one[:], 1.0).then_inc(made, 1)
            pool.memset(c["ones"][:], 1.0).then_inc(made, 1)
            pool.iota(c["iota_b"][:], pattern=[[1, NB]], base=0, channel_multiplier=0,
                      allow_small_or_imprecise_dtypes=True).then_inc(made, 1)
            pool.iota(c["node_no"][:], pattern=[[0, 4], [1, BN]], base=0, channel_multiplier=0,
                      allow_small_or_imprecise_dtypes=True).then_inc(made, 1)
            pool.iota(c["tile_no"][:], pattern=[[P, 8]], base=0, channel_multiplier=1,
                      allow_small_or_imprecise_dtypes=True).then_inc(made, 1)
            pool.wait_ge(made, 6)
            pool.affine_select(out=c["ident"][:], in_=zero[:], compare_op=ALU.not_equal, fill=1.0, base=0,
                               pattern=[[-1, P]], channel_multiplier=1).then_inc(made, 1)
            pool.affine_select(out=c["ident_far"][:], in_=zero[:], compare_op=ALU.not_equal, fill=-BIG, base=0,
                               pattern=[[-1, P]], channel_multiplier=1).then_inc(made, 1)
            pool.affine_select(out=c["tri"][:], in_=one[:], compare_op=ALU.is_gt, fill=0.0, base=0,
                               pattern=[[1, P]], channel_multiplier=-1).then_inc(made, 1)
            pool.affine_select(out=c["comp"][:], in_=zero[:], compare_op=ALU.is_gt, fill=1.0, base=0,
                               pattern=[[1, P]], channel_multiplier=-1).then_inc(made, 1)
            pool.wait_ge(made, 10)
            pool.affine_select(out=zero[:, 0:4], in_=one[:, 0:4], compare_op=ALU.is_ge, fill=0.0, base=0,
                               pattern=[[-32, 4]], channel_multiplier=1).then_inc(made, 1)
            pool.wait_ge(made, 11)
            pool.affine_select(out=c["head_rows"][:], in_=zero[:, 0:4], compare_op=ALU.is_ge, fill=0.0, base=31,
                               pattern=[[32, 4]], channel_multiplier=-1).then_inc(made, 1)
            pool.wait_ge(made, 12)
    return c


H0, F0 = 4, 64
TAB0 = 2 * F0 + 2 * H0


def second(k, g):
    return not isinstance(k, int) or k > 0


def edge_attention_0(nc, recs, tile_bucket, table, result, consts):
    GROUPS = SORT_TILES // GROUP
    RING = 4
    SPARE = RING * GROUP
    with Phase(nc) as ctx:
        def sb(name, shape, dt=F32):
            return ctx.enter_context(nc.sbuf_tensor(f"e0_{name}", shape, dt))

        def ps(name, shape):
            return ctx.enter_context(nc.psum_tensor(f"e0_{name}", shape, F32))

        def sem(name):
            return ctx.semaphore(f"e0_{name}")

        rec = sb("rec", [P, SORT_TILES, REC])
        other = sb("other", [P, SORT_TILES], I32)
        place_row = sb("place_row", [1, SORT_TILES], I32)
        row_f = sb("row_f", [1, SORT_TILES + 1])
        spare = sb("spare", [1, SORT_TILES])
        bucket_i = sb("bucket_i", [P, SORT_TILES], I32)
        bucket = sb("bucket", [P, SORT_TILES + 1])
        local = sb("local", [P, SORT_TILES])
        fresh = sb("fresh", [P, SORT_TILES])
        acc = sb("acc", [P, NB + SPARE, F0 + 2])
        acc_max = acc[:, 0:NB, F0 + 1]
        cur = sb("cur", [P, RING, GROUP, F0 + 2])
        index = [sb(f"index{g}", [P, GROUP], I32) for g in range(RING)]
        got = sb("got", [P, RING, GROUP, TAB0])
        part = sb("part", [P, 2, GROUP, H0])
        score = sb("score", [P, 2, GROUP, H0])
        far = sb("far", [P, 2, GROUP, H0, BN])
        mask = sb("mask", [P, 2, GROUP, P], BF16)
        msg = sb("msg", [P, RING, GROUP, F0 + 1])
        msg_r = sb("msg_r", [P, 2, GROUP, F0])
        low = sb("low", [P, 2, GROUP])
        run = sb("run", [P, RING, GROUP + 1])
        before = sb("before", [P, 2, GROUP])
        step = sb("step", [P, 2, GROUP])
        decay = sb("decay", [P, RING, GROUP])
        prob = sb("prob", [P, 2, GROUP, P])
        prob_t = sb("prob_t", [P, 2, GROUP, P])
        gmin = sb("gmin", [P, 1])
        grow = sb("grow", [1, P])
        ghead = sb("ghead", [1, H0])
        gall = sb("gall", [P, H0])
        gneg = sb("gneg", [P, 1])
        factor = sb("factor", [P, NB])
        den = sb("den", [P, NB])
        one_row = sb("one_row", [1, P])
        rows = [ps(f"rows{g}", [P, GROUP, P]) for g in range(2)]
        prob_tp = [ps(f"prob_tp{g}", [P, GROUP, P]) for g in range(2)]
        sums = [ps(f"sums{g}", [P, 512]) for g in range(2)]
        ident = consts["ident"]

        loaded = sem("loaded")
        ready = sem("ready")
        indexed = sem("indexed")
        issuing = sem("issuing")
        gathered = row_moves(consts, RING)
        laid = sem("laid")
        flushed = [sem(f"flushed{i}") for i in range(RING)]
        parted = sem("parted")
        placed = sem("placed")
        masked = sem("masked")
        turned_back = sem("turned_back")
        messaged = sem("messaged")
        rowed = sem("rowed")
        peaked = sem("peaked")
        decayed = sem("decayed")
        probed = sem("probed")
        flipped = sem("flipped")
        flipped_sb = sem("flipped_sb")
        summed = sem("summed")
        added = sem("added")
        final = sem("final")
        finish = sem("finish")
        final_pe = sem("final_pe")
        final_act = sem("final_act")
        stored = sem("stored")
        STEPS = 8

        def past(k, i, ring):
            return late(k, i, RING, ring)

        with nc.Block() as block:
            @block.sync
            def _(sp):
                sp.dma_start(rec[:].rearrange("p t r -> p (t r)"),
                             recs.rearrange("(p t) r -> p (t r)", p=P)).then_inc(loaded, 16)
                sp.dma_start(bucket_i[:], rows_of(tile_bucket[0:SORT_TILES], P)).then_inc(loaded, 16)

                def flush(k, i):
                    gi = RING * k + i
                    places = register_values(nc, mybir.EngineType.SP, place_row[0:1, bass.ds(gi * GROUP, GROUP)],
                                             NB + SPARE - 1)
                    sp.wait_ge(added, (gi + 1) * 5)
                    for j in range(GROUP):
                        sp.dma_start(acc[:, bass.ds(places[j], 1), :].rearrange("p a f -> p (a f)"),
                                     cur[:, i, j, :]).then_inc(flushed[i], 16)

                sp.wait_ge(laid, 7)
                pipeline(sp, [(flush, 0)], GROUPS, RING)
                sp.wait_ge(final, 9)
                for h in range(H0):
                    sp.dma_start(result[:, h * F0:(h + 1) * F0].rearrange("(b n) f -> n b f", n=BN),
                                 acc[BN * h:BN * h + BN, 0:NB - 1, 0:F0]).then_inc(stored, 16)
                sp.wait_ge(stored, 16 * H0)

            @block.gpsimd
            def _(pool):
                pool.iota(spare[:].rearrange("p (a b) -> p a b", b=SPARE), pattern=[[0, SORT_TILES // SPARE], [1, SPARE]],
                          base=NB, channel_multiplier=0, allow_small_or_imprecise_dtypes=True).then_inc(laid, 1)
                pool.wait_ge(ready, 4)

                def gather(k, i):
                    gi = RING * k + i
                    if past(k, i, RING):
                        pool.wait_ge(gathered[i], k * 16 * GROUP)
                    pool.tensor_copy(index[i][:], other[:, bass.ds(gi * GROUP, GROUP)]).then_inc(indexed, 1)
                    pool.wait_ge(indexed, gi + 1)
                    if past(k, i, RING):
                        pool.wait_ge(parted, (gi - RING) * 4 + 2)
                        pool.wait_ge(messaged, (gi - RING + 1) * GROUP)
                    pool.sem_inc(issuing, 1)
                    for j in range(GROUP):
                        pool.indirect_dma_start(
                            out=got[:, i, j, :], out_offset=None, in_=table,
                            in_offset=bass.IndirectOffsetOnAxis(ap=index[i][:, j:j + 1], axis=0),
                        ).then_inc(gathered[i], 16)

                pipeline(pool, [(gather, 0)], GROUPS, RING)

            @block.tensor
            def _(pe):
                def turn(k, i):
                    gi, b = RING * k + i, i % 2
                    pe.wait_ge(placed, gi + 1)
                    if past(k, i, 2):
                        pe.wait_ge(probed, (gi - 1) * GROUP)
                    for j in range(GROUP):
                        mm = pe.transpose(rows[b][:, j, :], far[:, b, j, :, :].rearrange("p h n -> p (h n)"), ident[:])
                    mm.then_inc(rowed, 1)

                def flip(k, i):
                    gi, b = RING * k + i, i % 2
                    if past(k, i, 2):
                        pe.wait_ge(flipped_sb, gi - 1)
                    for j in range(GROUP):
                        pe.wait_ge(probed, gi * GROUP + j + 1)
                        mm = pe.transpose(prob_tp[b][:, j, :], prob[:, b, j, :], ident[:])
                    mm.then_inc(flipped, 1)

                def sum_up(k, i):
                    gi, b = RING * k + i, i % 2
                    pe.wait_ge(flipped_sb, gi + 1)
                    pe.wait_ge(messaged, (gi + 1) * GROUP)
                    if past(k, i, 2):
                        pe.wait_ge(added, (gi - 1) * 5)
                    for j in range(GROUP):
                        mm = pe.matmul(sums[b][:, j * (F0 + 1):(j + 1) * (F0 + 1)], prob_t[:, b, j, :],
                                       msg[:, i, j, :], start=True, stop=True)
                    mm.then_inc(summed, 1)

                pipeline(pe, [(sum_up, -2), (flip, -1), (turn, 1)], GROUPS, RING)
                pe.wait_ge(final, 1)
                pe.transpose(rows[0][0:1, 0, :], gmin[:], ident[:]).then_inc(final_pe, 1)
                pe.wait_ge(final, 4)
                pe.matmul(rows[1][:, 0, 0:H0], one_row[:], ghead[:], start=True, stop=True).then_inc(final_pe, 1)

            @block.scalar
            def _(act):
                act.wait_ge(ready, 10)

                def make_masks(k, i):
                    gi, b = RING * k + i, i % 2
                    if past(k, i, 2):
                        act.wait_ge(placed, gi - 1)
                    for j in range(GROUP):
                        act.activation(mask[:, b, j, :], consts["node_no"][:].rearrange("p h n -> p (h n)"), ACT.Square,
                                       bias=local[:, bass.ds(gi * GROUP + j, 1)]).then_inc(masked, 1)

                def exponentiate(k, i):
                    gi, b = RING * k + i, i % 2
                    act.wait_ge(peaked, gi * STEPS + 2 + GROUP)
                    if past(k, i, 2):
                        act.wait_ge(flipped, gi - 1)
                    for j in range(GROUP):
                        act.activation(prob[:, b, j, :], rows[b][:, j, :], ACT.Exp,
                                       bias=run[:, i, j + 1:j + 2]).then_inc(probed, 1)

                def make_decay(k, i):
                    gi, b = RING * k + i, i % 2
                    act.wait_ge(peaked, (gi + 1) * STEPS)
                    if past(k, i, RING):
                        act.wait_ge(added, (gi - 3) * 5)
                    act.activation(decay[:, i, :], step[:, b, :], ACT.Exp).then_inc(decayed, 1)

                def copy_weights(k, i):
                    gi, b = RING * k + i, i % 2
                    act.wait_ge(flipped, gi + 1)
                    if past(k, i, 2):
                        act.wait_ge(summed, gi - 1)
                    act.activation(prob_t[:, b, :, :], prob_tp[b][:, :, :], ACT.Copy).then_inc(flipped_sb, 1)

                def turn_back(k, i):
                    gi, b = RING * k + i, i % 2
                    act.wait_ge(gathered[i], (k + 1) * 16 * GROUP)
                    if past(k, i, 2):
                        act.wait_ge(messaged, (gi - 1) * GROUP)
                    for j in range(GROUP):
                        act.activation(msg_r[:, b, j, :], got[:, i, j, F0:2 * F0], ACT.Copy,
                                       scale=rec[:, bass.ds(gi * GROUP + j, 1), 3:4].rearrange("p a r -> p (a r)")
                                       ).then_inc(turned_back, 1)

                pipeline(act, [(turn_back, 2), (make_masks, 2), (exponentiate, 0), (copy_weights, -1), (make_decay, 0)], GROUPS, RING)
                act.wait_ge(final, 6)
                act.activation(factor[:], acc_max, ACT.Exp, bias=gneg[:], scale=-1.0).then_inc(final_act, 1)

            @block.vector
            def _(dve):
                dve.memset(acc[:, :, 0:F0 + 1], 0.0).then_inc(ready, 1)
                dve.memset(msg[:], 1.0).then_inc(ready, 1)
                dve.memset(acc[:, :, F0 + 1:], FLOOR).then_inc(ready, 1)
                dve.wait_ge(loaded, 32)
                dve.tensor_copy(other[:], rec[:, :, 1]).then_inc(ready, 1)
                dve.memset(bucket[:, 0:1], -1.0).then_inc(ready, 1)
                dve.tensor_copy(bucket[:, 1:], bucket_i[:]).then_inc(ready, 1)
                dve.memset(run[:], FLOOR).then_inc(ready, 1)
                dve.memset(one_row[:], 1.0).then_inc(ready, 1)
                dve.memset(cur[:], 0.0).then_inc(ready, 1)
                dve.wait_ge(ready, 9)
                dve.scalar_tensor_tensor(local[:], bucket[:, 1:], float(BN), rec[:, :, 0], ALU.mult,
                                         ALU.subtract).then_inc(ready, 1)
                dve.tensor_tensor(fresh[:], bucket[:, 1:], bucket[:, 0:SORT_TILES], ALU.not_equal).then_inc(ready, 1)
                dve.wait_ge(ready, 11)
                dve.tensor_scalar(fresh[:], fresh[:], 2 * FLOOR, -FLOOR, ALU.mult, ALU.add).then_inc(ready, 1)
                dve.memset(row_f[:, SORT_TILES:], -1.0).then_inc(laid, 1)
                dve.tensor_copy(row_f[:, 0:SORT_TILES], bucket[0:1, 1:]).then_inc(laid, 1)
                dve.wait_ge(laid, 3)
                dve.tensor_tensor(bucket[0:1, 1:], row_f[:, 0:SORT_TILES], spare[:], ALU.subtract).then_inc(laid, 1)
                dve.wait_ge(laid, 4)
                dve.tensor_tensor(row_f[:, 0:SORT_TILES], row_f[:, 0:SORT_TILES], row_f[:, 1:],
                                  ALU.not_equal).then_inc(laid, 1)
                dve.wait_ge(laid, 5)
                dve.tensor_tensor(row_f[:, 0:SORT_TILES], row_f[:, 0:SORT_TILES], bucket[0:1, 1:],
                                  ALU.mult).then_inc(laid, 1)
                dve.wait_ge(laid, 6)
                dve.tensor_tensor(place_row[:], row_f[:, 0:SORT_TILES], spare[:], ALU.add).then_inc(laid, 1)
                dve.wait_ge(laid, 7)
                dve.wait_ge(ready, 12)

                def attribute(gi, a, width):
                    return rec[:, bass.ds(gi * GROUP, GROUP), 2 + a:3 + a].to_broadcast([P, GROUP, width])

                def score_parts(k, i):
                    gi, b = RING * k + i, i % 2
                    dve.wait_ge(gathered[i], (k + 1) * 16 * GROUP)
                    if past(k, i, 2):
                        dve.wait_ge(placed, gi - 1)
                    dve.wait_ge(parted, 4 * gi)
                    dve.tensor_tensor(part[:, b, :, :], got[:, i, :, 2 * F0 + H0:], attribute(gi, 1, H0),
                                      ALU.mult).then_inc(parted, 1)
                    dve.tensor_tensor(score[:, b, :, :], got[:, i, :, 2 * F0:2 * F0 + H0], attribute(gi, 0, H0),
                                      ALU.mult).then_inc(parted, 1)

                def score_sum(k, i):
                    gi, b = RING * k + i, i % 2
                    dve.wait_ge(parted, gi * 4 + 2)
                    dve.tensor_tensor(part[:, b, :, :], part[:, b, :, :], score[:, b, :, :], ALU.add).then_inc(parted, 1)

                def leaky(k, i):
                    gi, b = RING * k + i, i % 2
                    dve.wait_ge(parted, gi * 4 + 3)
                    dve.scalar_tensor_tensor(score[:, b, :, :], part[:, b, :, :], 0.2, part[:, b, :, :], ALU.mult,
                                             ALU.max).then_inc(parted, 1)

                def place_scores(k, i):
                    gi, b = RING * k + i, i % 2
                    dve.wait_ge(masked, (gi + 1) * GROUP)
                    dve.wait_ge(parted, gi * 4 + 4)
                    if past(k, i, 2):
                        dve.wait_ge(rowed, gi - 1)
                    dve.scalar_tensor_tensor(
                        far[:, b, :, :, :], mask[:, b, :, :].rearrange("p j (h n) -> p j h n", h=H0), -BIG,
                        score[:, b, :, :].unsqueeze(3).to_broadcast([P, GROUP, H0, BN]), ALU.mult,
                        ALU.add).then_inc(placed, 1)

                def message(k, i):
                    gi, b = RING * k + i, i % 2
                    dve.wait_ge(turned_back, (gi + 1) * GROUP)
                    if past(k, i, RING):
                        dve.wait_ge(summed, gi - 3)
                    for j in range(GROUP):
                        dve.scalar_tensor_tensor(msg[:, i, j, 0:F0], got[:, i, j, 0:F0],
                                                 rec[:, bass.ds(gi * GROUP + j, 1), 2:3].rearrange("p a r -> p (a r)"),
                                                 msg_r[:, b, j, :], ALU.mult, ALU.add).then_inc(messaged, 1)

                def peak(k, i):
                    gi, b = RING * k + i, i % 2
                    dve.wait_ge(rowed, gi + 1)
                    dve.wait_ge(peaked, gi * STEPS)
                    dve.tensor_reduce(low[:, b, :], rows[b][:, :, :], AX.X, ALU.max, negate=True).then_inc(peaked, 1)
                    if past(k, i, RING):
                        dve.wait_ge(probed, (gi - 3) * GROUP)
                        dve.wait_ge(added, (gi - 3) * 5)
                    dve.tensor_copy(run[:, i, 0:1], run[:, (i - 1) % RING, GROUP:]).then_inc(peaked, 1)

                def settle(j):
                    def stage(k, i):
                        gi, b = RING * k + i, i % 2
                        dve.wait_ge(peaked, gi * STEPS + 2 + j)
                        dve.scalar_tensor_tensor(run[:, i, j + 1:j + 2], run[:, i, j:j + 1],
                                                 fresh[:, bass.ds(gi * GROUP + j, 1)], low[:, b, j:j + 1],
                                                 ALU.max, ALU.min).then_inc(peaked, 1)
                    return stage, 0

                def look_back(k, i):
                    gi, b = RING * k + i, i % 2
                    dve.wait_ge(peaked, gi * STEPS + 1 + GROUP)
                    dve.scalar_tensor_tensor(before[:, b, :], fresh[:, bass.ds(gi * GROUP, GROUP)], 2.0,
                                             run[:, i, 0:GROUP], ALU.mult, ALU.max).then_inc(peaked, 1)

                def move(k, i):
                    gi, b = RING * k + i, i % 2
                    dve.wait_ge(peaked, gi * STEPS + 3 + GROUP)
                    if past(k, i, 2):
                        dve.wait_ge(decayed, gi - 1)
                    dve.tensor_tensor(step[:, b, :], run[:, i, 1:], before[:, b, :], ALU.subtract).then_inc(peaked, 1)

                def add(j):
                    def stage(k, i):
                        gi, b = RING * k + i, i % 2
                        if j == 0:
                            dve.wait_ge(summed, gi + 1)
                            dve.wait_ge(decayed, gi + 1)
                            if past(k, i, RING):
                                dve.wait_ge(flushed[i], k * 16 * GROUP)
                        dve.wait_ge(added, gi * 5 + j)
                        dve.scalar_tensor_tensor(cur[:, i, j, 0:F0 + 1],
                                                 cur[:, (i - (j == 0)) % RING, (j - 1) % GROUP, 0:F0 + 1],
                                                 decay[:, i, j:j + 1], sums[b][:, j * (F0 + 1):(j + 1) * (F0 + 1)],
                                                 ALU.mult, ALU.add).then_inc(added, 1)
                        if j == GROUP - 1:
                            dve.wait_ge(peaked, (gi + 1) * STEPS)
                            dve.tensor_copy(cur[:, i, :, F0 + 1], run[:, i, 1:]).then_inc(added, 1)
                    return stage, -2

                pipeline(dve, [(place_scores, 1), (peak, 0), (score_parts, 2), settle(0), (message, 1), settle(1),
                               (score_sum, 2), add(0), settle(2), (leaky, 2), add(1), settle(3), add(2),
                               (look_back, 0), add(3), (move, 0)], GROUPS, RING)

                for i in range(RING):
                    dve.wait_ge(flushed[i], 16 * SORT_TILES // RING)
                dve.tensor_reduce(gmin[:], acc_max[:, 0:NB - 1], AX.X, ALU.min).then_inc(final, 1)
                dve.wait_ge(final_pe, 1)
                dve.tensor_copy(grow[:], rows[0][0:1, 0, :]).then_inc(final, 1)
                dve.wait_ge(final, 2)
                dve.tensor_reduce(ghead[:], grow[:].rearrange("p (h n) -> p h n", h=H0), AX.X, ALU.min).then_inc(final, 1)
                dve.wait_ge(final, 3)
                dve.sem_inc(final, 1)
                dve.wait_ge(final_pe, 2)
                dve.tensor_tensor(gall[:], rows[1][:, 0, 0:H0], consts["head_rows"][:], ALU.mult).then_inc(final, 1)
                dve.wait_ge(final, 5)
                dve.tensor_reduce(gneg[:], gall[:], AX.X, ALU.add).then_inc(final, 1)
                dve.wait_ge(final_act, 1)
                z = acc[:, 0:NB, F0:F0 + 1].rearrange("p b a -> p (b a)")
                dve.tensor_tensor(den[:], z, factor[:], ALU.mult).then_inc(final, 1)
                dve.wait_ge(final, 7)
                dve.tensor_scalar(den[:], den[:], 1e-10, None, ALU.add).then_inc(final, 1)
                dve.wait_ge(final, 8)
                dve.reciprocal(den[:], den[:]).then_inc(finish, 1)
                dve.wait_ge(finish, 1)
                dve.tensor_tensor(den[:], den[:], factor[:], ALU.mult).then_inc(finish, 1)
                dve.wait_ge(finish, 2)
                dve.tensor_tensor(acc[:, 0:NB, 0:F0], acc[:, 0:NB, 0:F0],
                                  den[:].unsqueeze(2).to_broadcast([P, NB, F0]), ALU.mult).then_inc(final, 1)


PAIRS = NT // 2


def over_tiles(eng, first, body):
    with eng.Fori(first, PAIRS) as k:
        body(k, 0)
        body(k, 1)
    body(PAIRS, 0)


def normal_factors(nc, tag, stats, scale, shift):
    with Phase(nc) as ctx:
        def sb(name):
            return ctx.enter_context(nc.sbuf_tensor(f"{tag}_{name}", [P, NT], F32))

        total, gap, squares, spread = sb("total"), sb("gap"), sb("squares"), sb("spread")
        done = ctx.semaphore(f"{tag}_done")
        rooted = ctx.semaphore(f"{tag}_rooted")
        mean_e, dev_e, mean_o, dev_o = (stats[:, :, i] for i in (1, 2, 4, 5))
        with nc.Block() as block:
            @block.vector
            def _(dve):
                dve.tensor_tensor(total[:], mean_e, mean_o, ALU.add).then_inc(done, 1)
                dve.tensor_tensor(gap[:], mean_e, mean_o, ALU.subtract).then_inc(done, 1)
                dve.tensor_tensor(squares[:], dev_e, dev_o, ALU.add).then_inc(done, 1)
                dve.wait_ge(done, 3)
                dve.scalar_tensor_tensor(gap[:], gap[:], 0.25, gap[:], ALU.mult, ALU.mult).then_inc(done, 1)
                dve.wait_ge(done, 4)
                dve.scalar_tensor_tensor(squares[:], squares[:], 1.0 / D, gap[:], ALU.mult, ALU.add).then_inc(done, 1)
                dve.wait_ge(done, 5)
                dve.tensor_scalar(squares[:], squares[:], EPS, None, ALU.add).then_inc(done, 1)
                dve.wait_ge(rooted, 1)
                dve.reciprocal(scale[:], spread[:]).then_inc(done, 1)
                dve.wait_ge(done, 7)
                dve.scalar_tensor_tensor(shift[:], total[:], -0.5, scale[:], ALU.mult, ALU.mult).then_inc(done, 1)
                dve.wait_ge(done, 8)

            @block.scalar
            def _(act):
                act.wait_ge(done, 6)
                act.activation(spread[:], squares[:], ACT.Sqrt).then_inc(rooted, 1)


def first_stats(nc, x, xs, stats):
    with Phase(nc) as ctx:
        x_in, measured = ctx.semaphore("x_in"), ctx.semaphore("x_stats")
        with nc.Block() as block:
            @block.sync
            def _(sp):
                sp.dma_start(xs[:], x.rearrange("(t p) d -> p t d", p=P)).then_inc(x_in, 16)

            @block.vector
            def _(dve):
                dve.wait_ge(x_in, 16)
                for t in range(NT):
                    dve.bn_stats(stats[:, t, :], xs[:, t, :]).then_inc(measured, 1)
                dve.wait_ge(measured, NT)


def node_pass_0(nc, xs, scale, shift, w, table, xn_t, mix, mix_bias, consts):
    with Phase(nc) as ctx:
        def sb(name, shape, dt=F32):
            return ctx.enter_context(nc.sbuf_tensor(f"a_{name}", shape, dt))

        def ps(name, shape):
            return ctx.enter_context(nc.psum_tensor(f"a_{name}", shape, F32))

        def sem(name):
            return ctx.semaphore(f"a_{name}")

        w_edge = sb("w_edge", [P, 2, TAB0])
        w_dir = sb("w_dir", [F0, 2, D])
        heads_t = sb("heads_t", [F0, H0])
        w_kv = sb("w_kv", [P, 2, 2 * D])
        b_kv = sb("b_kv", [P, 2 * D])
        w_q = sb("w_q", [P, 2, D])
        b_q = sb("b_q", [P, 2])
        b_qm = sb("b_qm", [P, 2, P])
        w_fc = sb("w_fc", [P, 2, D])
        b_fc = sb("b_fc", [P, D])
        xn = sb("xn", [P, 2, D])
        xt = sb("xt", [P, 2, 2, P])
        tab = sb("tab", [P, 2, TAB0])
        kv = sb("kv", [P, 2, 2 * D])
        vk_bd = sb("vk_bd", [P, 2, P])
        inner = sb("inner", [P, 2, D])
        turned_p = [ps(f"turned{j}", [P, 2, P]) for j in range(2)]
        tab_p = [ps(f"tab{j}", [P, 512]) for j in range(2)]
        kv_p = [ps(f"kv{j}", [P, 512]) for j in range(2)]
        vk_p = [ps(f"vk{j}", [P, 512]) for j in range(2)]

        loaded = sem("loaded")
        weighed_pe, weighed = sem("weighed_pe"), sem("weighed")
        normed = sem("normed")
        turned = sem("turned")
        copied = sem("copied")
        tabled = sem("tabled")
        tabled_sb = sem("tabled_sb")
        keyed = sem("keyed")
        keyed_sb = sem("keyed_sb")
        summed = sem("summed")
        out_tab = [sem(f"out_tab{j}") for j in range(2)]
        out_xt = [sem(f"out_xt{j}") for j in range(2)]
        end, end_pe = sem("end"), sem("end_pe")

        with nc.Block() as block:
            @block.sync
            def _(sp):
                def both(ap):
                    return ap.rearrange("(c p) n -> p c n", p=P)

                sp.dma_start(w_edge[:, :, 0:F0], both(w["edge_f_t"])).then_inc(loaded, 16)
                sp.dma_start(w_edge[:, :, F0:2 * F0], both(w["edge_r_t"])).then_inc(loaded, 16)
                sp.dma_start(w_dir[:, 0, :], w["edge_f"]).then_inc(loaded, 16)
                sp.dma_start(w_dir[:, 1, :], w["edge_r"]).then_inc(loaded, 16)
                sp.dma_start(heads_t[:], w["edge_heads_t"]).then_inc(loaded, 16)
                sp.dma_start(w_kv[:, :, 0:D], both(w["mix0_k_t"])).then_inc(loaded, 16)
                sp.dma_start(w_kv[:, :, D:], both(w["mix0_v_t"])).then_inc(loaded, 16)
                sp.dma_start(b_kv[:, 0:D], rows_of(w["mix0_bk"], P)).then_inc(loaded, 16)
                sp.dma_start(b_kv[:, D:], rows_of(w["mix0_bv"], P)).then_inc(loaded, 16)
                sp.dma_start(w_q[:], both(w["mix0_q"])).then_inc(loaded, 16)
                with nc.allow_non_contiguous_dma(reason="a bias column"):
                    sp.dma_start(b_q[:], w["mix0_bq"].rearrange("(c p) -> p c", p=P)).then_inc(loaded, 16)
                sp.dma_start(w_fc[:], both(w["mix0_fc_t"])).then_inc(loaded, 16)
                sp.dma_start(b_fc[:], rows_of(w["mix0_bfc"], P)).then_inc(loaded, 16)

                def store(k, j):
                    t = 2 * k + j
                    sp.wait_ge(copied, t + 1)
                    sp.dma_start(xn_t[bass.ds(t, 1), :, :].rearrange("a p n -> (a p) n"),
                                 xt[:, j, :, :].rearrange("p c n -> p (c n)")).then_inc(out_xt[j], 16)
                    sp.wait_ge(tabled_sb, t + 1)
                    sp.dma_start(table[bass.ds(t * P, P), :], tab[:, j, :]).then_inc(out_tab[j], 16)

                over_tiles(sp, 0, store)
                for j in range(2):
                    sp.wait_ge(out_xt[j], 16 * (PAIRS + 1 - j))
                    sp.wait_ge(out_tab[j], 16 * (PAIRS + 1 - j))

            @block.scalar
            def _(act):
                def norm(k, j):
                    t = 2 * k + j
                    if second(k, j):
                        act.wait_ge(turned, t - 1)
                    act.activation(xn[:, j, :], xs[:, bass.ds(t, 1), :].rearrange("p a d -> p (a d)"), ACT.Identity,
                                   bias=shift[:, bass.ds(t, 1)], scale=scale[:, bass.ds(t, 1)]).then_inc(normed, 1)

                norm(0, 0)
                norm(0, 1)
                over_tiles(act, 1, norm)

            @block.tensor
            def _(pe):
                pe.wait_ge(loaded, 208)
                for i in range(2):
                    for c in range(2):
                        mm = pe.matmul(tab_p[0][:, (2 * i + c) * H0:(2 * i + c + 1) * H0],
                                       w_dir[:, i, c * P:(c + 1) * P], heads_t[:], start=True, stop=True)
                mm.then_inc(weighed_pe, 1)
                pe.wait_ge(weighed, 1)

                def turn(k, j):
                    t = 2 * k + j
                    pe.wait_ge(normed, t + 1)
                    if second(k, j):
                        pe.wait_ge(copied, t - 1)
                    for c in range(2):
                        mm = pe.transpose(turned_p[j][:, c, :], xn[:, j, c * P:(c + 1) * P], consts["ident"][:])
                    mm.then_inc(turned, 1)

                def project(k, j):
                    t = 2 * k + j
                    pe.wait_ge(copied, t + 1)
                    if second(k, j):
                        pe.wait_ge(keyed_sb, t - 1)
                        pe.wait_ge(tabled_sb, t - 1)
                    for c in range(2):
                        mm = pe.matmul(tab_p[j][:, 0:TAB0], xt[:, j, c, :], w_edge[:, c, :], start=c == 0, stop=c == 1)
                    mm.then_inc(tabled, 1)
                    for c in range(2):
                        mm = pe.matmul(kv_p[j][:], xt[:, j, c, :], w_kv[:, c, :], start=c == 0, stop=c == 1)
                    mm.then_inc(keyed, 1)

                def sum_up(k, j, rows=P, first=False, last=False):
                    t = 2 * k + j
                    pe.wait_ge(keyed_sb, t + 1)
                    for c in range(2):
                        mm = pe.matmul(vk_p[c][:, 0:P], kv[0:rows, j, D + c * P:D + (c + 1) * P],
                                       kv[0:rows, j, c * P:(c + 1) * P], start=first, stop=last)
                    mm.then_inc(summed, 1)

                turn(0, 0)
                turn(0, 1)
                project(0, 0)
                turn(1, 0)
                project(0, 1)
                sum_up(0, 0, first=True)
                with pe.Fori(1, PAIRS) as k:
                    turn(k, 1)
                    project(k, 0)
                    sum_up(k - 1, 1)
                    turn(k + 1, 0)
                    project(k, 1)
                    sum_up(k, 0)
                project(PAIRS, 0)
                sum_up(PAIRS - 1, 1)
                sum_up(PAIRS, 0, rows=LAST, last=True)
                pe.wait_ge(end, 1)
                for c in range(2):
                    mm = pe.matmul(kv_p[c][:, 0:D], vk_bd[:, c, :], w_fc[:, c, :], start=True, stop=True)
                mm.then_inc(end_pe, 1)
                pe.wait_ge(end, 2)
                for i in range(2):
                    for c in range(2):
                        pe.matmul(tab_p[i][:, 0:D], w_q[:, c, i * P:(i + 1) * P], inner[:, c, :],
                                  start=c == 0, stop=c == 1)
                for c in range(2):
                    mm = pe.matmul(turned_p[0][:].rearrange("p a n -> p (a n)"), b_qm[:, c, :], inner[:, c, :],
                                   start=c == 0, stop=c == 1)
                mm.then_inc(end_pe, 1)

            @block.vector
            def _(dve):
                dve.wait_ge(weighed_pe, 1)
                for i in range(2):
                    for c in range(2):
                        op = dve.tensor_copy(w_edge[:, c, 2 * F0 + i * H0:2 * F0 + (i + 1) * H0],
                                             tab_p[0][:, (2 * i + c) * H0:(2 * i + c + 1) * H0])
                op.then_inc(weighed, 1)

                def copy(k, j):
                    t = 2 * k + j
                    dve.wait_ge(turned, t + 1)
                    if second(k, j):
                        dve.wait_ge(keyed, t - 1)
                        dve.wait_ge(out_xt[j], k * 16)
                    dve.tensor_copy(xt[:, j, :, :], turned_p[j][:, :, :]).then_inc(copied, 1)

                def evacuate(k, j):
                    t = 2 * k + j
                    dve.wait_ge(tabled, t + 1)
                    if second(k, j):
                        dve.wait_ge(out_tab[j], k * 16)
                        dve.wait_ge(summed, t - 1)
                    dve.tensor_copy(tab[:, j, :], tab_p[j][:, 0:TAB0]).then_inc(tabled_sb, 1)
                    dve.wait_ge(keyed, t + 1)
                    dve.tensor_tensor(kv[:, j, :], kv_p[j][:], b_kv[:], ALU.add).then_inc(keyed_sb, 1)

                copy(0, 0)
                copy(0, 1)
                evacuate(0, 0)
                copy(1, 0)
                evacuate(0, 1)
                with dve.Fori(1, PAIRS) as k:
                    copy(k, 1)
                    evacuate(k, 0)
                    copy(k + 1, 0)
                    evacuate(k, 1)
                evacuate(PAIRS, 0)
                dve.wait_ge(summed, NT)
                for c in range(2):
                    op = dve.scalar_tensor_tensor(
                        vk_bd[:, c, :].rearrange("p (h d) -> p h d", h=4),
                        vk_p[c][:, 0:P].rearrange("p (h d) -> p h d", h=4), 1.0 / N,
                        consts["head_rows"][:].unsqueeze(2).to_broadcast([P, 4, BN]), ALU.mult, ALU.mult)
                for c in range(2):
                    op2 = dve.tensor_copy(b_qm[:, c, :], b_q[:, c:c + 1].to_broadcast([P, P]))
                op2.then_inc(end, 1)
                dve.wait_ge(end_pe, 1)
                for c in range(2):
                    op = dve.tensor_copy(inner[:, c, :], kv_p[c][:, 0:D])
                op.then_inc(end, 1)
                dve.wait_ge(end_pe, 2)
                for i in range(2):
                    dve.tensor_copy(mix[:, i, :], tab_p[i][:, 0:D])
                dve.tensor_tensor(mix_bias[:], turned_p[0][:].rearrange("p a n -> p (a n)"), b_fc[:],
                                  ALU.add).then_inc(end, 1)
                dve.wait_ge(end, 3)


H1, G1 = 8, 64
HG = H1 * G1


def residual_0(nc, xs, stats, xn_t, edge_out, mix, mix_bias):
    with Phase(nc) as ctx:
        def sem(name):
            return ctx.semaphore(f"b_{name}")

        xt = ctx.enter_context(nc.sbuf_tensor("b_xt", [P, 2, 2, P], F32))
        edge = ctx.enter_context(nc.sbuf_tensor("b_edge", [P, 2, D], F32))
        out_p = [ctx.enter_context(nc.psum_tensor(f"b_out{j}", [P, 512], F32)) for j in range(2)]
        in_x = [sem(f"in_x{j}") for j in range(2)]
        in_e = [sem(f"in_e{j}") for j in range(2)]
        mapped = sem("mapped")
        added = sem("added")
        measured = sem("measured")

        with nc.Block() as block:
            @block.sync
            def _(sp):
                def load(k, j):
                    t = 2 * k + j
                    if second(k, j):
                        sp.wait_ge(added, 3 * (t - 1))
                    sp.dma_start(xt[:, j, :, :].rearrange("p c n -> p (c n)"),
                                 xn_t[bass.ds(t, 1), :, :].rearrange("a p n -> (a p) n")).then_inc(in_x[j], 16)
                    sp.dma_start(edge[:, j, :], edge_out[bass.ds(t * P, P), :]).then_inc(in_e[j], 16)

                load(0, 0)
                load(0, 1)
                over_tiles(sp, 1, load)

            @block.tensor
            def _(pe):
                def project(k, j):
                    t = 2 * k + j
                    pe.wait_ge(in_x[j], (k + 1) * 16)
                    if second(k, j):
                        pe.wait_ge(added, 3 * (t - 1))
                    for c in range(2):
                        mm = pe.matmul(out_p[j][:, 0:D], xt[:, j, c, :], mix[:, c, :], start=c == 0, stop=c == 1)
                    mm.then_inc(mapped, 1)

                project(0, 0)
                project(0, 1)
                over_tiles(pe, 1, project)

            @block.vector
            def _(dve):
                def accumulate(k, j):
                    t = 2 * k + j
                    row = xs[:, bass.ds(t, 1), :].rearrange("p a d -> p (a d)")
                    dve.wait_ge(in_e[j], (k + 1) * 16)
                    dve.tensor_tensor(edge[:, j, :], edge[:, j, :], mix_bias[:], ALU.add).then_inc(added, 1)
                    dve.wait_ge(mapped, t + 1)
                    dve.tensor_tensor(row, row, out_p[j][:, 0:D], ALU.add).then_inc(added, 1)
                    dve.wait_ge(added, 3 * t + 2)
                    dve.tensor_tensor(row, row, edge[:, j, :], ALU.add).then_inc(added, 1)
                    dve.wait_ge(added, 3 * t + 3)
                    dve.bn_stats(stats[:, bass.ds(t, 1), :].rearrange("p a d -> p (a d)"), row).then_inc(measured, 1)

                over_tiles(dve, 0, accumulate)
                dve.wait_ge(measured, NT)


def slice_weights(nc, xs, scale, shift, w, weights, tokens, consts):
    with Phase(nc) as ctx:
        def sb(name, shape, dt=F32):
            return ctx.enter_context(nc.sbuf_tensor(f"s_{name}", shape, dt))

        def ps(name, shape):
            return ctx.enter_context(nc.psum_tensor(f"s_{name}", shape, F32))

        def sem(name):
            return ctx.semaphore(f"s_{name}")

        w_x_t = sb("w_x_t", [P, 4, D])
        w_slice = sb("w_slice", [P, P])
        b_x = sb("b_x", [P, 4])
        b_xm = sb("b_xm", [P, 4, P])
        b_slice = sb("b_slice", [P, G1])
        temp = sb("temp", [P, H1])
        itemp = sb("itemp", [P, H1])
        w_l = sb("w_l", [P, 2, HG])
        b_l = sb("b_l", [P, HG])
        xn = sb("xn", [P, FOUR, D + 1])
        xt = sb("xt", [P, 2, 2, P])
        logit = sb("logit", [P, 2, HG])
        peak = sb("peak", [P, 2, H1])
        expd = sb("expd", [P, 2, HG])
        total = sb("total", [P, 2, H1])
        inverse = sb("inverse", [P, 2, H1])
        weight = sb("weight", [P, 2, HG])
        turned_p = [ps(f"turned{j}", [P, 2, P]) for j in range(2)]
        logit_p = [ps(f"logit{j}", [P, HG]) for j in range(2)]
        token_p = [ps(f"token{q}", [P, 512]) for q in range(4)]

        loaded, cleared = sem("loaded"), sem("cleared")
        built, built_pe = sem("built"), sem("built_pe")
        normed, turned, copied = sem("normed"), sem("turned"), sem("copied")
        scored = sem("scored")
        biased = sem("biased")
        exped = sem("exped")
        shared = sem("shared")
        summed = sem("summed")
        out_w = [sem(f"out_w{j}") for j in range(2)]

        def heads(ap):
            return ap.rearrange("p (h g) -> p h g", h=H1)

        def per_head(ap):
            return ap.unsqueeze(2).to_broadcast([P, H1, G1])

        with nc.Block() as block:
            @block.sync
            def _(sp):
                sp.dma_start(w_x_t[:], w["ffn0_x_t"].rearrange("(q p) n -> p q n", p=P)).then_inc(loaded, 16)
                sp.wait_ge(cleared, 1)
                sp.dma_start(w_slice[0:G1, 0:G1], w["ffn0_slice"]).then_inc(loaded, 16)
                sp.dma_start(w_slice[G1:, G1:], w["ffn0_slice"]).then_inc(loaded, 16)
                with nc.allow_non_contiguous_dma(reason="bias columns"):
                    sp.dma_start(b_x[:], w["ffn0_bx"].rearrange("(q p) -> p q", p=P)).then_inc(loaded, 16)
                sp.dma_start(b_slice[:], rows_of(w["ffn0_bslice"], P)).then_inc(loaded, 16)
                sp.dma_start(temp[:], rows_of(w["ffn0_temp"], P)).then_inc(loaded, 16)

                def store(k, j):
                    t = 2 * k + j
                    sp.wait_ge(shared, 3 * t + 3)
                    sp.dma_start(weights[bass.ds(t * P, P), :], weight[:, j, :]).then_inc(out_w[j], 16)

                over_tiles(sp, 0, store)
                for j in range(2):
                    sp.wait_ge(out_w[j], 16 * (PAIRS + 1 - j))

            @block.scalar
            def _(act):
                def norm(k, i):
                    t = FOUR * k + i
                    if late(k, i, FOUR, FOUR):
                        act.wait_ge(summed, t - 3)
                    act.activation(xn[:, i, 0:D], xs[:, bass.ds(t, 1), :].rearrange("p a d -> p (a d)"), ACT.Identity,
                                   bias=shift[:, bass.ds(t, 1)], scale=scale[:, bass.ds(t, 1)]).then_inc(normed, 1)

                def exponential(k, i):
                    t, b = FOUR * k + i, i % 2
                    act.wait_ge(biased, 3 * t + 3)
                    if late(k, i, FOUR, 2):
                        act.wait_ge(shared, 3 * t - 3)
                    act.activation(expd[:, b, :], logit[:, b, :], ACT.Exp).then_inc(exped, 1)

                act.wait_ge(cleared, 2)
                pipeline(act, [(norm, 3), (exponential, 1)], NT, FOUR)

            @block.tensor
            def _(pe):
                pe.wait_ge(loaded, 96)
                for c in range(2):
                    for q in range(4):
                        mm = pe.matmul(logit_p[c][:, q * P:(q + 1) * P], w_x_t[:, q, c * P:(c + 1) * P], w_slice[:],
                                       start=True, stop=True)
                pe.wait_ge(built, 1)
                for q in range(4):
                    mm = pe.matmul(token_p[0][:, q * P:(q + 1) * P], b_xm[:, q, :], w_slice[:], start=True, stop=True)
                mm.then_inc(built_pe, 1)
                pe.wait_ge(built, 2)

                def turn(k, i):
                    t, b = FOUR * k + i, i % 2
                    pe.wait_ge(normed, t + 1)
                    if late(k, i, FOUR, 2):
                        pe.wait_ge(copied, t - 1)
                    for c in range(2):
                        mm = pe.transpose(turned_p[b][:, c, :], xn[:, i, c * P:(c + 1) * P], consts["ident"][:])
                    mm.then_inc(turned, 1)

                def project(k, i):
                    t, b = FOUR * k + i, i % 2
                    pe.wait_ge(copied, t + 1)
                    if late(k, i, FOUR, 2):
                        pe.wait_ge(biased, 3 * (t - 2) + 1)
                    for c in range(2):
                        mm = pe.matmul(logit_p[b][:], xt[:, b, c, :], w_l[:, c, :], start=c == 0, stop=c == 1)
                    mm.then_inc(scored, 1)

                def sum_up(k, i):
                    t, b = FOUR * k + i, i % 2
                    first = isinstance(k, int) and t == 0
                    last = isinstance(k, int) and t == NT - 1
                    rows = LAST if last else P
                    pe.wait_ge(shared, 3 * t + 3)
                    for q in range(4):
                        mm = pe.matmul(token_p[q][:, 0:D + 1], weight[0:rows, b, q * P:(q + 1) * P], xn[0:rows, i, :],
                                       start=first, stop=last)
                    mm.then_inc(summed, 1)

                pipeline(pe, [(project, 1), (turn, 2), (sum_up, 0)], NT, FOUR)

            @block.vector
            def _(dve):
                dve.memset(w_slice[:], 0.0).then_inc(cleared, 1)
                dve.memset(xn[:, :, D:], 1.0).then_inc(cleared, 1)
                dve.wait_ge(loaded, 96)
                op = dve.tensor_copy(b_xm[:], b_x[:].unsqueeze(2).to_broadcast([P, 4, P]))
                dve.tensor_scalar(temp[:], temp[:], 0.1, 5.0, ALU.max, ALU.min).then_inc(cleared, 1)
                dve.wait_ge(cleared, 3)
                dve.reciprocal(itemp[:], temp[:]).then_inc(cleared, 1)
                dve.wait_ge(cleared, 4)
                dve.sem_inc(built, 1)
                dve.wait_ge(built_pe, 1)
                for c in range(2):
                    dve.tensor_tensor(heads(w_l[:, c, :]), heads(logit_p[c][:]), per_head(itemp[:]), ALU.mult)
                dve.tensor_tensor(heads(b_l[:]), heads(token_p[0][:]),
                                  b_slice[:].unsqueeze(1).to_broadcast([P, H1, G1]), ALU.add).then_inc(cleared, 1)
                dve.wait_ge(cleared, 5)
                dve.tensor_tensor(heads(b_l[:]), heads(b_l[:]), per_head(itemp[:]), ALU.mult).then_inc(built, 1)
                dve.wait_ge(built, 2)

                def copy(k, i):
                    t, b = FOUR * k + i, i % 2
                    dve.wait_ge(turned, t + 1)
                    if late(k, i, FOUR, 2):
                        dve.wait_ge(scored, t - 1)
                    dve.tensor_copy(xt[:, b, :, :], turned_p[b][:, :, :]).then_inc(copied, 1)

                def before(k, i):
                    t, b = FOUR * k + i, i % 2
                    dve.wait_ge(scored, t + 1)
                    if late(k, i, FOUR, 2):
                        dve.wait_ge(exped, t - 1)
                    dve.tensor_tensor(logit[:, b, :], logit_p[b][:], b_l[:], ALU.add).then_inc(biased, 1)
                    dve.wait_ge(biased, 3 * t + 1)
                    dve.tensor_reduce(peak[:, b, :], heads(logit[:, b, :]), AX.X, ALU.max).then_inc(biased, 1)
                    dve.wait_ge(biased, 3 * t + 2)
                    dve.tensor_tensor(heads(logit[:, b, :]), heads(logit[:, b, :]), per_head(peak[:, b, :]),
                                      ALU.subtract).then_inc(biased, 1)

                def after(k, i):
                    t, b = FOUR * k + i, i % 2
                    dve.wait_ge(exped, t + 1)
                    dve.tensor_reduce(total[:, b, :], heads(expd[:, b, :]), AX.X, ALU.add).then_inc(shared, 1)
                    dve.wait_ge(shared, 3 * t + 1)
                    dve.reciprocal(inverse[:, b, :], total[:, b, :]).then_inc(shared, 1)
                    dve.wait_ge(shared, 3 * t + 2)
                    if late(k, i, FOUR, 2):
                        dve.wait_ge(out_w[b], (k * (FOUR // 2) + i // 2) * 16)
                        dve.wait_ge(summed, t - 1)
                    dve.tensor_tensor(heads(weight[:, b, :]), heads(expd[:, b, :]), per_head(inverse[:, b, :]),
                                      ALU.mult).then_inc(shared, 1)

                pipeline(dve, [(after, 0), (before, 1), (copy, 2)], NT, FOUR)
                dve.wait_ge(summed, NT)
                for q in range(4):
                    op = dve.tensor_copy(tokens[:, q, :], token_p[q][:, 0:D + 1])
                op.then_inc(built, 1)
                dve.wait_ge(built, 3)


def slice_attention(nc, w, tokens, out_map, consts):
    with Phase(nc) as ctx:
        def sb(name, shape, dt=F32):
            return ctx.enter_context(nc.sbuf_tensor(f"t_{name}", shape, dt))

        w_fx = sb("w_fx", [P, 2, HG])
        b_fx = sb("b_fx", [P, HG])
        w_qkv = sb("w_qkv", [P, 3, P])
        w_out = sb("w_out", [P, 4, D])
        blocks = sb("blocks", [P, 2])
        norm = sb("norm", [P, 4])
        token_t = sb("token_t", [P, 4, 2, P])
        token = sb("token", [P, 4, P])
        tok_t = sb("tok_t", [P, 4, P])
        q_t = sb("q_t", [P, 4, P])
        k_t = sb("k_t", [P, 4, P])
        v = sb("v", [P, 4, P])
        score = sb("score", [P, 4, G1])
        peak = sb("peak", [P, 4])
        total = sb("total", [P, 4])
        attn = sb("attn", [P, 4, P])
        attn_t = sb("attn_t", [P, 4, P])
        out_t = sb("out_t", [P, 4, P])
        wide = ctx.enter_context(nc.psum_tensor("t_wide", [P, 4, 2, P], F32))
        pb = [ctx.enter_context(nc.psum_tensor(f"t_p{i}", [P, 4, P], F32)) for i in range(4)]
        loaded = ctx.semaphore("t_loaded")
        pe_done = ctx.semaphore("t_pe_done")
        dve_done = ctx.semaphore("t_dve_done")
        act_done = ctx.semaphore("t_act_done")
        inverted = ctx.semaphore("t_inverted")

        with nc.Block() as block:
            @block.sync
            def _(sp):
                sp.dma_start(w_fx[:], w["ffn0_fx"].rearrange("(c p) n -> p c n", p=P)).then_inc(loaded, 16)
                sp.dma_start(b_fx[:], rows_of(w["ffn0_bfx"], P)).then_inc(loaded, 16)
                sp.dma_start(w_out[:], w["ffn0_out"].rearrange("(q p) n -> p q n", p=P)).then_inc(loaded, 16)
                sp.wait_ge(dve_done, 1)
                for i, name in enumerate(("ffn0_q", "ffn0_k", "ffn0_v")):
                    sp.dma_start(w_qkv[0:G1, i, 0:G1], w[name]).then_inc(loaded, 16)
                    sp.dma_start(w_qkv[G1:, i, G1:], w[name]).then_inc(loaded, 16)

            @block.tensor
            def _(pe):
                for q in range(4):
                    for c in range(2):
                        mm = pe.transpose(wide[:, q, c, :], tokens[:, q, c * P:(c + 1) * P], consts["ident"][:])
                mm.then_inc(pe_done, 1)
                pe.wait_ge(loaded, 144)
                pe.wait_ge(dve_done, 5)
                for q in range(4):
                    for c in range(2):
                        mm = pe.matmul(pb[0][:, q, :], token_t[:, q, c, :], w_fx[:, c, q * P:(q + 1) * P],
                                       start=c == 0, stop=c == 1)
                mm.then_inc(pe_done, 1)
                pe.wait_ge(dve_done, 8)
                for q in range(4):
                    mm = pe.transpose(pb[1][:, q, :], token[:, q, :], consts["ident"][:])
                mm.then_inc(pe_done, 1)
                pe.wait_ge(dve_done, 9)
                for q in range(4):
                    pe.matmul(pb[2][:, q, :], w_qkv[:, 0, :], tok_t[:, q, :], start=True, stop=True)
                for q in range(4):
                    mm = pe.matmul(pb[3][:, q, :], w_qkv[:, 1, :], tok_t[:, q, :], start=True, stop=True)
                for q in range(4):
                    mm = pe.matmul(pb[0][:, q, :], tok_t[:, q, :], w_qkv[:, 2, :], start=True, stop=True)
                mm.then_inc(pe_done, 1)
                pe.wait_ge(dve_done, 12)
                for q in range(4):
                    mm = pe.matmul(pb[1][:, q, :], q_t[:, q, :], k_t[:, q, :], start=True, stop=True)
                mm.then_inc(pe_done, 1)
                pe.wait_ge(dve_done, 20)
                for q in range(4):
                    mm = pe.transpose(pb[2][:, q, :], attn[:, q, :], consts["ident"][:])
                mm.then_inc(pe_done, 1)
                pe.wait_ge(dve_done, 21)
                for q in range(4):
                    mm = pe.matmul(pb[3][:, q, :], v[:, q, :], attn_t[:, q, :], start=True, stop=True)
                mm.then_inc(pe_done, 1)
                pe.wait_ge(dve_done, 22)
                for q in range(4):
                    mm = pe.matmul(wide[:, q, :, :].rearrange("p c n -> p (c n)"), out_t[:, q, :], w_out[:, q, :],
                                   start=True, stop=True)
                mm.then_inc(pe_done, 1)

            @block.scalar
            def _(act):
                act.wait_ge(dve_done, 16)
                act.activation(score[:], score[:], ACT.Exp, scale=float(G1) ** -0.5).then_inc(act_done, 1)

            @block.vector
            def _(dve):
                steps = [0]

                def done(op):
                    steps[0] += 1
                    op.then_inc(dve_done, 1)
                    dve.wait_ge(dve_done, steps[0])

                done(dve.memset(w_qkv[:], 0.0))
                done(dve.tensor_reduce(blocks[:], consts["head_rows"][:].rearrange("p (a b) -> p a b", b=2), AX.X,
                                       ALU.add))
                done(dve.tensor_copy(norm[:], tokens[:, :, D]))
                done(dve.memset(attn[:], 0.0))
                dve.wait_ge(pe_done, 1)
                done(dve.tensor_copy(token_t[:], wide[:]))
                dve.wait_ge(pe_done, 2)
                for q in range(4):
                    op = dve.scalar_tensor_tensor(token[:, q, :], b_fx[:, q * P:(q + 1) * P], norm[:, q:q + 1],
                                                  pb[0][:, q, :], ALU.mult, ALU.add)
                done(op)
                done(dve.tensor_scalar(norm[:], norm[:], 1e-5, None, ALU.add))
                dve.reciprocal(total[:], norm[:]).then_inc(inverted, 1)
                dve.wait_ge(inverted, 1)
                for q in range(4):
                    op = dve.scalar_tensor_tensor(
                        token[:, q, :].rearrange("p (a c) -> p a c", a=2), token[:, q, :].rearrange("p (a c) -> p a c", a=2),
                        total[:, q:q + 1], blocks[:].unsqueeze(2).to_broadcast([P, 2, G1]), ALU.mult, ALU.mult)
                done(op)
                dve.wait_ge(pe_done, 3)
                done(dve.tensor_copy(tok_t[:], pb[1][:]))
                dve.wait_ge(pe_done, 4)
                done(dve.tensor_copy(q_t[:], pb[2][:]))
                done(dve.tensor_copy(k_t[:], pb[3][:]))
                done(dve.tensor_copy(v[:], pb[0][:]))
                dve.wait_ge(pe_done, 5)
                done(dve.tensor_copy(score[0:G1, :, :], pb[1][0:G1, :, 0:G1]))
                done(dve.tensor_copy(score[G1:, :, :], pb[1][G1:, :, G1:]))
                done(dve.tensor_reduce(peak[:], score[:], AX.X, ALU.max))
                done(dve.tensor_tensor(score[:], score[:], peak[:].unsqueeze(2).to_broadcast([P, 4, G1]), ALU.subtract))
                dve.wait_ge(act_done, 1)
                done(dve.tensor_reduce(total[:], score[:], AX.X, ALU.add))
                done(dve.reciprocal(total[:], total[:]))
                for half in (slice(0, G1), slice(G1, P)):
                    done(dve.tensor_tensor(attn[half, :, half], score[half, :, :],
                                           total[half, :].unsqueeze(2).to_broadcast([G1, 4, G1]), ALU.mult))
                dve.wait_ge(pe_done, 6)
                done(dve.tensor_copy(attn_t[:], pb[2][:]))
                dve.wait_ge(pe_done, 7)
                done(dve.tensor_copy(out_t[:], pb[3][:]))
                dve.wait_ge(pe_done, 8)
                done(dve.tensor_copy(out_map[:], wide[:].rearrange("p q c n -> p q (c n)")))


def residual_slices(nc, xs, stats, weights, out_map, b_out, x_rows, consts):
    with Phase(nc) as ctx:
        def sb(name, shape, dt=F32):
            return ctx.enter_context(nc.sbuf_tensor(f"c_{name}", shape, dt))

        def sem(name):
            return ctx.semaphore(f"c_{name}")

        bias = sb("bias", [P, D])
        weight = sb("weight", [P, 2, HG])
        weight_t = sb("weight_t", [P, 2, 4, P])
        turned_p = [ctx.enter_context(nc.psum_tensor(f"c_turned{j}", [P, 4, P], F32)) for j in range(2)]
        out_p = [ctx.enter_context(nc.psum_tensor(f"c_out{j}", [P, 512], F32)) for j in range(2)]
        in_b = sem("in_b")
        in_w = [sem(f"in_w{j}") for j in range(2)]
        turned, copied, mapped = sem("turned"), sem("copied"), sem("mapped")
        added, measured = sem("added"), sem("measured")
        stored = sem("stored")

        with nc.Block() as block:
            @block.sync
            def _(sp):
                sp.dma_start(bias[:], rows_of(b_out, P)).then_inc(in_b, 16)

                def load(k, j):
                    t = 2 * k + j
                    if second(k, j):
                        sp.wait_ge(turned, t - 1)
                    sp.dma_start(weight[:, j, :], weights[bass.ds(t * P, P), :]).then_inc(in_w[j], 16)

                def store(k, j):
                    t = 2 * k + j
                    sp.wait_ge(added, 2 * t + 2)
                    sp.dma_start(x_rows[bass.ds(t * P, P), :],
                                 xs[:, bass.ds(t, 1), :].rearrange("p a d -> p (a d)")).then_inc(stored, 16)

                load(0, 0)
                load(0, 1)
                with sp.Fori(1, PAIRS) as k:
                    for j in range(2):
                        load(k, j)
                        store(k - 1, j)
                load(PAIRS, 0)
                for t in range(NT - 3, NT):
                    store(t // 2, t % 2)
                sp.wait_ge(stored, 16 * NT)

            @block.tensor
            def _(pe):
                def turn(k, j):
                    t = 2 * k + j
                    pe.wait_ge(in_w[j], (k + 1) * 16)
                    if second(k, j):
                        pe.wait_ge(copied, t - 1)
                    for q in range(4):
                        mm = pe.transpose(turned_p[j][:, q, :], weight[:, j, q * P:(q + 1) * P], consts["ident"][:])
                    mm.then_inc(turned, 1)

                def project(k, j):
                    t = 2 * k + j
                    pe.wait_ge(copied, t + 1)
                    if second(k, j):
                        pe.wait_ge(added, 2 * (t - 1))
                    for q in range(4):
                        mm = pe.matmul(out_p[j][:, 0:D], weight_t[:, j, q, :], out_map[:, q, :], start=q == 0, stop=q == 3)
                    mm.then_inc(mapped, 1)

                turn(0, 0)
                turn(0, 1)
                project(0, 0)
                turn(1, 0)
                project(0, 1)
                with pe.Fori(1, PAIRS) as k:
                    turn(k, 1)
                    project(k, 0)
                    turn(k + 1, 0)
                    project(k, 1)
                project(PAIRS, 0)

            @block.scalar
            def _(act):
                def copy(k, j):
                    t = 2 * k + j
                    act.wait_ge(turned, t + 1)
                    if second(k, j):
                        act.wait_ge(mapped, t - 1)
                    act.activation(weight_t[:, j, :, :], turned_p[j][:, :, :], ACT.Copy).then_inc(copied, 1)

                copy(0, 0)
                copy(0, 1)
                over_tiles(act, 1, copy)

            @block.vector
            def _(dve):
                dve.wait_ge(in_b, 16)

                def accumulate(k, j):
                    t = 2 * k + j
                    row = xs[:, bass.ds(t, 1), :].rearrange("p a d -> p (a d)")
                    dve.wait_ge(mapped, t + 1)
                    dve.tensor_tensor(row, row, out_p[j][:, 0:D], ALU.add).then_inc(added, 1)
                    dve.wait_ge(added, 2 * t + 1)
                    dve.tensor_tensor(row, row, bias[:], ALU.add).then_inc(added, 1)
                    dve.wait_ge(added, 2 * t + 2)
                    dve.bn_stats(stats[:, bass.ds(t, 1), :].rearrange("p a d -> p (a d)"), row).then_inc(measured, 1)

                over_tiles(dve, 0, accumulate)
                dve.wait_ge(measured, NT)


H2, F2 = 8, 32
V1 = F2 + 1
TAB1 = D + H2 * V1


def node_pass_1(nc, xs, scale, shift, w, table, query_t, mix_query_t, mix_sums, consts):
    with Phase(nc) as ctx:
        def sb(name, shape, dt=F32):
            return ctx.enter_context(nc.sbuf_tensor(f"f_{name}", shape, dt))

        def ps(name, shape):
            return ctx.enter_context(nc.psum_tensor(f"f_{name}", shape, F32))

        def sem(name):
            return ctx.semaphore(f"f_{name}")

        w_q = sb("w_q", [P, 2, 2 * D])
        w_kv = sb("w_kv", [P, 2, 2 * D])
        w_mkv = sb("w_mkv", [P, 2, 2 * D])
        b_q = sb("b_q", [P, 2])
        b_qs = sb("b_qs", [P, 2])
        b_mq = sb("b_mq", [P, 2])
        b_kv = sb("b_kv", [P, 2 * D])
        b_mkv = sb("b_mkv", [P, 2 * D])
        xn = sb("xn", [P, 2, D])
        xt = sb("xt", [P, 2, 2, P])
        tab = sb("tab", [P, 2, TAB1])
        qt = sb("qt", [P, 2, P // BN, 2, BN])
        no_query = sb("no_query", [P, 2 * BN])
        key = sb("key", [P, 2, D])
        key_low = sb("key_low", [P, 2, D])
        key_exp = sb("key_exp", [P, 2, D])
        value = sb("value", [P, 2, 2, P + 1])
        mq = sb("mq", [P, 2, 2, P])
        mq_low = sb("mq_low", [P, 2, 2, P])
        mq_exp = sb("mq_exp", [P, 2, 2, P])
        turned_p = [ps(f"turned{j}", [P, 2, P]) for j in range(2)]
        q_p, mq_p = ps("q_p", [P, 2, P]), ps("mq_p", [P, 2, P])
        kv_p, mkv_p = ps("kv", [P, 2 * D]), ps("mkv", [P, 2 * D])
        sum_p = [ps(f"sum{c}", [P, 512]) for c in range(2)]
        QSCALE = float(F2) ** -0.5

        loaded, ready = sem("loaded"), sem("ready")
        cleared = sem("cleared")
        normed, turned, copied = sem("normed"), sem("turned"), sem("copied")
        keyed, mixed, asked = sem("keyed"), sem("mixed"), sem("asked")
        tabled = sem("tabled")
        mix_steps = sem("mix_steps")
        key_exped = sem("key_exped")
        ask_steps = sem("ask_steps")
        mq_exped = sem("mq_exped")
        queried = sem("queried")
        summed = sem("summed")
        out_t = [sem(f"out_t{j}") for j in range(2)]
        out_q = [sem(f"out_q{j}") for j in range(2)]
        out_m = [sem(f"out_m{j}") for j in range(2)]

        with nc.Block() as block:
            @block.sync
            def _(sp):
                def both(ap):
                    return ap.rearrange("(c p) n -> p c n", p=P)

                sp.dma_start(w_q[:, :, 0:D], both(w["edge1_q"])).then_inc(loaded, 16)
                sp.dma_start(w_q[:, :, D:], both(w["mix1_q"])).then_inc(loaded, 16)
                sp.dma_start(w_kv[:, :, 0:D], both(w["edge1_k"])).then_inc(loaded, 16)
                sp.dma_start(w_kv[:, :, D:], both(w["edge1_v"])).then_inc(loaded, 16)
                sp.dma_start(w_mkv[:, :, 0:D], both(w["mix1_k"])).then_inc(loaded, 16)
                sp.dma_start(w_mkv[:, :, D:], both(w["mix1_v"])).then_inc(loaded, 16)
                with nc.allow_non_contiguous_dma(reason="bias columns"):
                    sp.dma_start(b_q[:], w["edge1_bq"].rearrange("(c p) -> p c", p=P)).then_inc(loaded, 16)
                    sp.dma_start(b_mq[:], w["mix1_bq"].rearrange("(c p) -> p c", p=P)).then_inc(loaded, 16)
                sp.dma_start(b_kv[:, 0:D], rows_of(w["edge1_bk"], P)).then_inc(loaded, 16)
                sp.dma_start(b_kv[:, D:], rows_of(w["edge1_bv"], P)).then_inc(loaded, 16)
                sp.dma_start(b_mkv[:, 0:D], rows_of(w["mix1_bk"], P)).then_inc(loaded, 16)
                sp.dma_start(b_mkv[:, D:], rows_of(w["mix1_bv"], P)).then_inc(loaded, 16)

                def store(k, j):
                    t = 2 * k + j
                    sp.wait_ge(tabled, 2 * t + 2)
                    sp.dma_start(table[bass.ds(t * P, P), :], tab[:, j, :]).then_inc(out_t[j], 16)
                    sp.wait_ge(queried, 2 * t + 2)
                    sp.dma_start(query_t[bass.ds(t * (P // BN), P // BN), :, :].rearrange("b p n -> p b n"),
                                 qt[:, j, :, :, :].rearrange("p b c n -> p b (c n)")).then_inc(out_q[j], 16)
                    sp.wait_ge(ask_steps, 5 * t + 5)
                    sp.dma_start(mix_query_t[bass.ds(t, 1), :, :].rearrange("a p n -> (a p) n"),
                                 mq[:, j, :, :].rearrange("p c n -> p (c n)")).then_inc(out_m[j], 16)

                over_tiles(sp, 0, store)
                sp.wait_ge(cleared, 1)
                sp.dma_start(query_t[NB - 1, :, :], no_query[:]).then_inc(cleared, 16)
                sp.wait_ge(cleared, 17)
                for j in range(2):
                    for s in (out_t[j], out_q[j], out_m[j]):
                        sp.wait_ge(s, 16 * (PAIRS + 1 - j))

            @block.scalar
            def _(act):
                def norm(k, j):
                    t = 2 * k + j
                    if second(k, j):
                        act.wait_ge(turned, t - 1)
                    act.activation(xn[:, j, :], xs[:, bass.ds(t, 1), :].rearrange("p a d -> p (a d)"), ACT.Identity,
                                   bias=shift[:, bass.ds(t, 1)], scale=scale[:, bass.ds(t, 1)]).then_inc(normed, 1)

                def finish(k, j):
                    t = 2 * k + j
                    act.wait_ge(mix_steps, 4 * t + 3)
                    act.activation(key_exp[:, j, :], key_low[:, j, :], ACT.Exp).then_inc(key_exped, 1)
                    act.wait_ge(asked, t + 1)
                    if second(k, j):
                        act.wait_ge(out_q[j], k * 16)
                    for c in range(2):
                        act.activation(qt[:, j, :, c, :], q_p[:, c, :].rearrange("p (b n) -> p b n", n=BN), ACT.Identity, bias=b_qs[:, c:c + 1],
                                       scale=QSCALE).then_inc(queried, 1)
                    act.wait_ge(ask_steps, 5 * t + 4)
                    act.activation(mq_exp[:, j, :, :], mq_low[:, j, :, :], ACT.Exp).then_inc(mq_exped, 1)

                norm(0, 0)
                norm(0, 1)
                act.wait_ge(ready, 1)
                finish(0, 0)
                norm(1, 0)
                finish(0, 1)
                with act.Fori(1, PAIRS) as k:
                    norm(k, 1)
                    finish(k, 0)
                    norm(k + 1, 0)
                    finish(k, 1)
                finish(PAIRS, 0)

            @block.tensor
            def _(pe):
                pe.wait_ge(loaded, 192)

                def turn(k, j):
                    t = 2 * k + j
                    pe.wait_ge(normed, t + 1)
                    if second(k, j):
                        pe.wait_ge(copied, t - 1)
                    for c in range(2):
                        mm = pe.transpose(turned_p[j][:, c, :], xn[:, j, c * P:(c + 1) * P], consts["ident"][:])
                    mm.then_inc(turned, 1)

                def project(k, j):
                    t = 2 * k + j
                    late = second(k, j)
                    pe.wait_ge(copied, t + 1)
                    if late or j:
                        pe.wait_ge(tabled, 2 * t)
                    for c in range(2):
                        mm = pe.matmul(kv_p[:], xt[:, j, c, :], w_kv[:, c, :], start=c == 0, stop=c == 1)
                    mm.then_inc(keyed, 1)
                    if late or j:
                        pe.wait_ge(mix_steps, 4 * t - 2)
                    for c in range(2):
                        mm = pe.matmul(mkv_p[:], xt[:, j, c, :], w_mkv[:, c, :], start=c == 0, stop=c == 1)
                    mm.then_inc(mixed, 1)
                    if late or j:
                        pe.wait_ge(queried, 2 * t)
                        pe.wait_ge(ask_steps, 5 * (t - 1) + 4)
                    for o in range(4):
                        for c in range(2):
                            mm = pe.matmul((q_p, mq_p)[o // 2][:, o % 2, :], w_q[:, c, o * P:(o + 1) * P],
                                           xt[:, j, c, :], start=c == 0, stop=c == 1)
                    mm.then_inc(asked, 1)

                def sum_up(k, j, rows=P, first=False, last=False):
                    t = 2 * k + j
                    pe.wait_ge(mix_steps, 4 * t + 4)
                    for c in range(2):
                        mm = pe.matmul(sum_p[c][:, 0:P + 1], key[0:rows, j, c * P:(c + 1) * P], value[0:rows, j, c, :],
                                       start=first, stop=last)
                    mm.then_inc(summed, 1)

                turn(0, 0)
                turn(0, 1)
                project(0, 0)
                turn(1, 0)
                project(0, 1)
                sum_up(0, 0, first=True)
                with pe.Fori(1, PAIRS) as k:
                    turn(k, 1)
                    project(k, 0)
                    sum_up(k - 1, 1)
                    turn(k + 1, 0)
                    project(k, 1)
                    sum_up(k, 0)
                project(PAIRS, 0)
                sum_up(PAIRS - 1, 1)
                sum_up(PAIRS, 0, rows=LAST, last=True)

            @block.vector
            def _(dve):
                for j in range(2):
                    v = tab[:, j, D:].rearrange("p (h f) -> p h f", h=H2)
                    dve.memset(v[:, :, F2:], 1.0)
                dve.memset(value[:, :, :, P:], 1.0)
                dve.memset(no_query[:], 0.0).then_inc(cleared, 1)
                dve.wait_ge(loaded, 192)
                dve.tensor_scalar(b_qs[:], b_q[:], QSCALE, None, ALU.mult).then_inc(ready, 1)

                def copy(k, j):
                    t = 2 * k + j
                    dve.wait_ge(turned, t + 1)
                    if second(k, j):
                        dve.wait_ge(asked, t - 1)
                    dve.tensor_copy(xt[:, j, :, :], turned_p[j][:, :, :]).then_inc(copied, 1)

                def evacuate(k, j):
                    t = 2 * k + j
                    late = second(k, j)
                    dve.wait_ge(keyed, t + 1)
                    if late:
                        dve.wait_ge(out_t[j], k * 16)
                    dve.tensor_tensor(tab[:, j, 0:D], kv_p[:, 0:D], b_kv[:, 0:D], ALU.add).then_inc(tabled, 1)
                    v = tab[:, j, D:].rearrange("p (h f) -> p h f", h=H2)
                    dve.tensor_tensor(v[:, :, 0:F2], kv_p[:, D:].rearrange("p (h f) -> p h f", h=H2),
                                      b_kv[:, D:].rearrange("p (h f) -> p h f", h=H2), ALU.add).then_inc(tabled, 1)
                    dve.wait_ge(mixed, t + 1)
                    if late:
                        dve.wait_ge(summed, t - 1)
                        dve.wait_ge(key_exped, t - 1)
                    dve.tensor_tensor(key[:, j, :], mkv_p[:, 0:D], b_mkv[:, 0:D], ALU.add).then_inc(mix_steps, 1)
                    dve.tensor_tensor(value[:, j, :, 0:P], mkv_p[:, D:].rearrange("p (c n) -> p c n", c=2),
                                      b_mkv[:, D:].rearrange("p (c n) -> p c n", c=2), ALU.add).then_inc(mix_steps, 1)
                    dve.wait_ge(mix_steps, 4 * t + 1)
                    dve.tensor_scalar(key_low[:, j, :], key[:, j, :], 0.0, None, ALU.min).then_inc(mix_steps, 1)
                    dve.wait_ge(asked, t + 1)
                    if late:
                        dve.wait_ge(out_m[j], k * 16)
                        dve.wait_ge(mq_exped, t - 1)
                    for c in range(2):
                        dve.tensor_scalar(mq[:, j, c, :], mq_p[:, c, :], b_mq[:, c:c + 1], 0.0, ALU.add,
                                          ALU.max).then_inc(ask_steps, 1)
                    for c in range(2):
                        dve.tensor_scalar(mq_low[:, j, c, :], mq_p[:, c, :], b_mq[:, c:c + 1], 0.0, ALU.add,
                                          ALU.min).then_inc(ask_steps, 1)
                    dve.wait_ge(key_exped, t + 1)
                    dve.wait_ge(mix_steps, 4 * t + 3)
                    dve.scalar_tensor_tensor(key[:, j, :], key[:, j, :], 0.0, key_exp[:, j, :], ALU.max,
                                             ALU.add).then_inc(mix_steps, 1)
                    dve.wait_ge(mq_exped, t + 1)
                    dve.wait_ge(ask_steps, 5 * t + 2)
                    dve.tensor_tensor(mq[:, j, :, :], mq[:, j, :, :], mq_exp[:, j, :, :], ALU.add).then_inc(ask_steps, 1)

                copy(0, 0)
                copy(0, 1)
                evacuate(0, 0)
                copy(1, 0)
                evacuate(0, 1)
                with dve.Fori(1, PAIRS) as k:
                    copy(k, 1)
                    evacuate(k, 0)
                    copy(k + 1, 0)
                    evacuate(k, 1)
                evacuate(PAIRS, 0)
                dve.wait_ge(summed, NT)
                for c in range(2):
                    dve.tensor_tensor(mix_sums[:, c, 0:P].rearrange("p (h d) -> p h d", h=4),
                                      sum_p[c][:, 0:P].rearrange("p (h d) -> p h d", h=4),
                                      consts["head_rows"][:].unsqueeze(2).to_broadcast([P, 4, F2]), ALU.mult)
                    op = dve.tensor_tensor(mix_sums[:, c, P:], consts["head_rows"][:],
                                           sum_p[c][:, P:P + 1].to_broadcast([P, 4]), ALU.mult)
                op.then_inc(ready, 1)
                dve.wait_ge(ready, 2)


def edge_attention_1(nc, recs, tile_bucket, table, query_t, result, consts):
    G = 2
    GROUPS = SORT_TILES // G
    RING = 8
    SPARE = 4 * G
    with Phase(nc) as ctx:
        def sb(name, shape, dt=F32):
            return ctx.enter_context(nc.sbuf_tensor(f"e1_{name}", shape, dt))

        def ps(name, shape):
            return ctx.enter_context(nc.psum_tensor(f"e1_{name}", shape, F32))

        def sem(name):
            return ctx.semaphore(f"e1_{name}")

        other = sb("other", [P, SORT_TILES], I32)
        plan = sb("plan", [1, GROUPS + RING, 2 * G], I32)
        row_f = sb("row_f", [1, SORT_TILES + 1])
        spare = sb("spare", [1, SORT_TILES])
        bucket_i = other
        bucket = sb("bucket", [P, SORT_TILES + 1])
        local = sb("local", [P, SORT_TILES])
        fresh = sb("fresh", [P, SORT_TILES])
        acc = sb("acc", [P, NB + SPARE, 2, V1])
        cur = sb("cur", [P, 4, G, 2, V1])
        query = sb("query", [P, RING, G, 2, BN])
        index = [sb(f"index{i}", [P, G], I32) for i in range(RING)]
        got = sb("got", [P, RING, G, TAB1])
        rec = got[:].rearrange("p a b n -> p (a b n)")[:, 0:SORT_TILES * REC].rearrange("p (t r) -> p t r", r=REC)
        key_t = sb("key_t", [P, 2, G, 2, P])
        spread = sb("spread", [P, 2, G, 2, 4, BN])
        mask = sb("mask", [P, 2, G, P], BF16)
        low = sb("low", [P, 2, G, 2])
        run = sb("run", [P, 4, G + 1, 2])
        before = sb("before", [P, 2, G, 2])
        step = sb("step", [P, 2, G, 2])
        decay = sb("decay", [P, 4, G, 2])
        prob = sb("prob", [P, 2, G, 2, P])
        prob_t = sb("prob_t", [P, 2, G, 2, P])
        key_p = [ps(f"key{i}", [P, G, 2, P]) for i in range(2)]
        rows = [ps(f"rows{i}", [P, G, 2, P]) for i in range(2)]
        prob_p = [ps(f"prob{i}", [P, G, 2, P]) for i in range(2)]
        sums = [ps(f"sums{i}", [P, 512]) for i in range(2)]
        ident, ident_far = consts["ident"], consts["ident_far"]

        loaded, ready = sem("loaded"), sem("ready")
        flushed = [sem(f"flushed{i}") for i in range(4)]
        asked = [sem(f"asked{i}") for i in range(RING)]
        laid = sem("laid")
        indexed, issuing = sem("indexed"), sem("issuing")
        gathered = row_moves(consts, RING)
        turned = sem("turned")
        copied = sem("copied")
        masked = sem("masked")
        diagonal = sem("diagonal")
        scored = sem("scored")
        peaked = sem("peaked")
        decayed = sem("decayed")
        probed = sem("probed")
        flipped = sem("flipped")
        flipped_sb = sem("flipped_sb")
        summed = sem("summed")
        added = sem("added")
        final, stored = sem("final"), sem("stored")
        STEPS = 4 + G

        def slots(ap):
            return ap.rearrange("p a b -> p (a b)")

        def past(k, i, ring):
            return late(k, i, RING, ring)

        with nc.Block() as block:
            @block.sync
            def _(sp):
                sp.dma_start(slots(rec), recs.rearrange("(p t) r -> p (t r)", p=P)).then_inc(loaded, 16)
                sp.dma_start(bucket_i[:], rows_of(tile_bucket[0:SORT_TILES], P)).then_inc(loaded, 16)
                def exchange(k, i, flush=True, fetch=True):
                    gi = RING * k + i
                    at = register_values(nc, mybir.EngineType.SP, plan[0:1, bass.ds(gi, 1), :].rearrange("p a n -> p (a n)"),
                                         NB + SPARE - 1)
                    if flush:
                        r = i % 4
                        sp.wait_ge(added, (gi - RING + 1) * 2 * G)
                        for j in range(G):
                            sp.dma_start(acc[:, bass.ds(at[j], 1), :, :].rearrange("p a c f -> p (a c f)"),
                                         cur[:, r, j, :, :].rearrange("p c f -> p (c f)")).then_inc(flushed[r], 16)
                    if fetch:
                        if flush:
                            sp.wait_ge(diagonal, (gi - RING + 1) * G)
                        for j in range(G):
                            sp.dma_start(query[:, i, j, :, :].rearrange("p c n -> p (c n)"),
                                         query_t[bass.ds(at[G + j], 1), :, :].rearrange("a p n -> (a p) n")
                                         ).then_inc(asked[i], 16)

                sp.wait_ge(ready, 10)
                for i in range(RING):
                    exchange(0, i, flush=False)
                with sp.Fori(1, GROUPS // RING) as k:
                    for i in range(RING):
                        exchange(k, i)
                for i in range(RING):
                    exchange(GROUPS // RING, i, fetch=False)
                sp.wait_ge(final, 3)
                for h in range(H2):
                    c, r = h // 4, h % 4
                    sp.dma_start(result[:, h * F2:(h + 1) * F2].rearrange("(b n) f -> n b f", n=BN),
                                 acc[BN * r:BN * r + BN, 0:NB - 1, c, 0:F2]).then_inc(stored, 16)
                sp.wait_ge(stored, 16 * H2)

            @block.gpsimd
            def _(pool):
                pool.iota(spare[:].rearrange("p (a b) -> p a b", b=SPARE), pattern=[[0, SORT_TILES // SPARE], [1, SPARE]],
                          base=NB, channel_multiplier=0, allow_small_or_imprecise_dtypes=True).then_inc(laid, 1)
                pool.wait_ge(ready, 7)

                def gather(k, i):
                    gi = RING * k + i
                    if past(k, i, RING):
                        pool.wait_ge(gathered[i], k * 16 * G)
                    pool.tensor_copy(index[i][:], other[:, bass.ds(gi * G, G)]).then_inc(indexed, 1)
                    pool.wait_ge(indexed, gi + 1)
                    if past(k, i, RING):
                        pool.wait_ge(summed, gi - RING + 1)
                        pool.sem_inc(issuing, 1)
                    else:
                        pool.sem_inc(issuing, 1)
                    for j in range(G):
                        pool.indirect_dma_start(
                            out=got[:, i, j, :], out_offset=None, in_=table,
                            in_offset=bass.IndirectOffsetOnAxis(ap=index[i][:, j:j + 1], axis=0),
                        ).then_inc(gathered[i], 16)

                pipeline(pool, [(gather, 0)], GROUPS, RING)

            @block.tensor
            def _(pe):
                def turn(k, i):
                    gi, b = RING * k + i, i % 2
                    pe.wait_ge(gathered[i], (k + 1) * 16 * G)
                    if past(k, i, 2):
                        pe.wait_ge(copied, gi - 1)
                    for j in range(G):
                        for c in range(2):
                            mm = pe.transpose(key_p[b][:, j, c, :], got[:, i, j, c * P:(c + 1) * P], ident[:])
                    mm.then_inc(turned, 1)

                def score(k, i):
                    gi, b = RING * k + i, i % 2
                    pe.wait_ge(copied, gi + 1)
                    pe.wait_ge(diagonal, (gi + 1) * G)
                    pe.wait_ge(masked, (gi + 1) * G)
                    if past(k, i, 2):
                        pe.wait_ge(probed, (gi - 1) * 2 * G)
                    for j in range(G):
                        for c in range(2):
                            pe.matmul(rows[b][:, j, c, :], spread[:, b, j, c, :, :].rearrange("p h n -> p (h n)"),
                                      key_t[:, b, j, c, :], start=True, stop=False)
                            mm = pe.matmul(rows[b][:, j, c, :], mask[:, b, j, :], ident_far[:], start=False, stop=True)
                    mm.then_inc(scored, 1)

                def flip(k, i):
                    gi, b = RING * k + i, i % 2
                    if past(k, i, 2):
                        pe.wait_ge(flipped_sb, gi - 1)
                    for j in range(G):
                        for c in range(2):
                            pe.wait_ge(probed, gi * 2 * G + 2 * j + c + 1)
                            mm = pe.transpose(prob_p[b][:, j, c, :], prob[:, b, j, c, :], ident[:])
                    mm.then_inc(flipped, 1)

                def sum_up(k, i):
                    gi, b = RING * k + i, i % 2
                    pe.wait_ge(flipped_sb, gi + 1)
                    if past(k, i, 2):
                        pe.wait_ge(added, (gi - 1) * 2 * G)
                    for j in range(G):
                        for h in range(H2):
                            c, r = h // 4, h % 4
                            at = (2 * j + c) * V1
                            mm = pe.matmul(sums[b][BN * r:BN * r + BN, at:at + V1],
                                           prob_t[:, b, j, c, BN * r:BN * r + BN],
                                           got[:, i, j, D + h * V1:D + (h + 1) * V1], start=True, stop=True)
                    mm.then_inc(summed, 1)

                pipeline(pe, [(score, 0), (flip, -1), (sum_up, -2), (turn, 2)], GROUPS, RING)

            @block.scalar
            def _(act):
                def copy_keys(k, i):
                    gi, b = RING * k + i, i % 2
                    act.wait_ge(turned, gi + 1)
                    if past(k, i, 2):
                        act.wait_ge(scored, gi - 1)
                    act.activation(key_t[:, b, :, :, :], key_p[b][:, :, :, :], ACT.Copy).then_inc(copied, 1)

                act.wait_ge(ready, 10)

                def make_masks(k, i):
                    gi, b = RING * k + i, i % 2
                    if past(k, i, 2):
                        act.wait_ge(scored, gi - 1)
                    for j in range(G):
                        act.activation(mask[:, b, j, :], consts["node_no"][:].rearrange("p h n -> p (h n)"), ACT.Square,
                                       bias=local[:, bass.ds(gi * G + j, 1)]).then_inc(masked, 1)

                def exponentiate(k, i):
                    gi, b = RING * k + i, i % 2
                    act.wait_ge(peaked, gi * STEPS + 2 + G)
                    if past(k, i, 2):
                        act.wait_ge(flipped, gi - 1)
                    for j in range(G):
                        for c in range(2):
                            act.activation(prob[:, b, j, c, :], rows[b][:, j, c, :], ACT.Exp,
                                           bias=run[:, i % 4, j + 1, c:c + 1]).then_inc(probed, 1)

                def make_decay(k, i):
                    gi, b = RING * k + i, i % 2
                    act.wait_ge(peaked, (gi + 1) * STEPS)
                    if past(k, i, 4):
                        act.wait_ge(added, (gi - 3) * 2 * G)
                    act.activation(decay[:, i % 4, :, :], step[:, b, :, :], ACT.Exp).then_inc(decayed, 1)

                def copy_weights(k, i):
                    gi, b = RING * k + i, i % 2
                    act.wait_ge(flipped, gi + 1)
                    if past(k, i, 2):
                        act.wait_ge(summed, gi - 1)
                    act.activation(prob_t[:, b, :, :, :], prob_p[b][:, :, :, :], ACT.Copy).then_inc(flipped_sb, 1)

                pipeline(act, [(copy_keys, 1), (copy_weights, -1), (exponentiate, 0), (make_masks, 2),
                               (make_decay, 0)], GROUPS, RING)

            @block.vector
            def _(dve):
                dve.memset(acc[:], 0.0).then_inc(ready, 1)
                dve.wait_ge(loaded, 32)
                dve.memset(bucket[:, 0:1], -1.0).then_inc(ready, 1)
                dve.tensor_copy(bucket[:, 1:], bucket_i[:]).then_inc(ready, 1)
                dve.memset(run[:], FLOOR).then_inc(ready, 1)
                dve.wait_ge(ready, 4)
                dve.scalar_tensor_tensor(local[:], bucket[:, 1:], float(BN), rec[:, :, 0], ALU.mult,
                                         ALU.subtract).then_inc(ready, 1)
                dve.tensor_tensor(fresh[:], bucket[:, 1:], bucket[:, 0:SORT_TILES], ALU.not_equal).then_inc(ready, 1)
                dve.tensor_copy(other[:], rec[:, :, 1]).then_inc(ready, 1)
                dve.wait_ge(ready, 7)
                dve.tensor_scalar(fresh[:], fresh[:], 2 * FLOOR, -FLOOR, ALU.mult, ALU.add).then_inc(ready, 1)
                dve.memset(plan[:], 0).then_inc(laid, 1)
                dve.memset(row_f[:, SORT_TILES:], -1.0).then_inc(laid, 1)
                dve.tensor_copy(row_f[:, 0:SORT_TILES], bucket[0:1, 1:]).then_inc(laid, 1)
                dve.wait_ge(laid, 4)
                dve.tensor_copy(plan[:, 0:GROUPS, G:], row_f[:, 0:SORT_TILES].rearrange("p (g j) -> p g j", j=G)).then_inc(laid, 1)
                dve.tensor_tensor(bucket[0:1, 1:], row_f[:, 0:SORT_TILES], spare[:], ALU.subtract).then_inc(laid, 1)
                dve.wait_ge(laid, 6)
                dve.tensor_tensor(row_f[:, 0:SORT_TILES], row_f[:, 0:SORT_TILES], row_f[:, 1:],
                                  ALU.not_equal).then_inc(laid, 1)
                dve.wait_ge(laid, 7)
                dve.tensor_tensor(row_f[:, 0:SORT_TILES], row_f[:, 0:SORT_TILES], bucket[0:1, 1:],
                                  ALU.mult).then_inc(laid, 1)
                dve.wait_ge(laid, 8)
                dve.tensor_tensor(plan[:, RING:, 0:G], row_f[:, 0:SORT_TILES].rearrange("p (g j) -> p g j", j=G),
                                  spare[:].rearrange("p (g j) -> p g j", j=G), ALU.add).then_inc(ready, 1)
                dve.memset(cur[:], 0.0).then_inc(ready, 1)
                dve.wait_ge(ready, 10)

                def spread_queries(j):
                    def stage(k, i):
                        gi, b = RING * k + i, i % 2
                        if j == 0 and past(k, i, 2):
                            dve.wait_ge(scored, gi - 1)
                        dve.wait_ge(asked[i], (k + 1) * 16 * G)
                        dve.tensor_tensor(spread[:, b, j, :, :, :],
                                          query[:, i, j, :, :].unsqueeze(2).to_broadcast([P, 2, 4, BN]),
                                          consts["head_rows"][:].unsqueeze(1).unsqueeze(3).to_broadcast([P, 2, 4, BN]),
                                          ALU.mult).then_inc(diagonal, 1)
                    return stage, 2

                def peak(k, i):
                    gi, b, r = RING * k + i, i % 2, i % 4
                    base = gi * STEPS
                    dve.wait_ge(scored, gi + 1)
                    dve.wait_ge(peaked, base)
                    dve.tensor_reduce(low[:, b, :, :], rows[b][:, :, :, :], AX.X, ALU.max, negate=True).then_inc(peaked, 1)
                    if past(k, i, 4):
                        dve.wait_ge(probed, (gi - 3) * 2 * G)
                    dve.tensor_copy(run[:, r, 0, :], run[:, (r - 1) % 4, G, :]).then_inc(peaked, 1)

                def settle(j):
                    def stage(k, i):
                        gi, b, r = RING * k + i, i % 2, i % 4
                        dve.wait_ge(peaked, gi * STEPS + 2 + j)
                        dve.scalar_tensor_tensor(run[:, r, j + 1, :], run[:, r, j, :],
                                                 fresh[:, bass.ds(gi * G + j, 1)], low[:, b, j, :],
                                                 ALU.max, ALU.min).then_inc(peaked, 1)
                    return stage, 0

                def look_back(k, i):
                    gi, b, r = RING * k + i, i % 2, i % 4
                    dve.wait_ge(peaked, gi * STEPS + 1 + G)
                    dve.scalar_tensor_tensor(before[:, b, :, :],
                                             fresh[:, bass.ds(gi * G, G)].unsqueeze(2).to_broadcast([P, G, 2]), 2.0,
                                             run[:, r, 0:G, :], ALU.mult, ALU.max).then_inc(peaked, 1)

                def move(k, i):
                    gi, b, r = RING * k + i, i % 2, i % 4
                    dve.wait_ge(peaked, gi * STEPS + 3 + G)
                    if past(k, i, 2):
                        dve.wait_ge(decayed, gi - 1)
                    dve.tensor_tensor(step[:, b, :, :], run[:, r, 1:, :], before[:, b, :, :],
                                      ALU.subtract).then_inc(peaked, 1)

                def add(j):
                    def stage(k, i):
                        gi, b, r = RING * k + i, i % 2, i % 4
                        if j == 0:
                            dve.wait_ge(summed, gi + 1)
                            dve.wait_ge(decayed, gi + 1)
                            if past(k, i, 4):
                                dve.wait_ge(flushed[r], (k * (RING // 4) + i // 4) * 16 * G)
                        dve.wait_ge(added, (gi * G + j) * 2)
                        for c in range(2):
                            at = (2 * j + c) * V1
                            dve.scalar_tensor_tensor(cur[:, r, j, c, :], cur[:, (r - (j == 0)) % 4, (j - 1) % G, c, :],
                                                     decay[:, r, j, c:c + 1], sums[b][:, at:at + V1], ALU.mult,
                                                     ALU.add).then_inc(added, 1)
                    return stage, -3

                pipeline(dve, [(peak, 0), add(0), settle(0), spread_queries(0), settle(1), (look_back, 0),
                               add(1), (move, 0), spread_queries(1)], GROUPS, RING)
                for i in range(4):
                    dve.wait_ge(flushed[i], 16 * SORT_TILES // 4)
                dve.tensor_scalar(acc[:, 0:NB, :, F2:], acc[:, 0:NB, :, F2:], 1e-30, None, ALU.max).then_inc(final, 1)
                dve.wait_ge(final, 1)
                dve.reciprocal(acc[:, 0:NB, :, F2:], acc[:, 0:NB, :, F2:]).then_inc(final, 1)
                dve.wait_ge(final, 2)
                dve.tensor_tensor(acc[:, 0:NB, :, 0:F2], acc[:, 0:NB, :, 0:F2],
                                  acc[:, 0:NB, :, F2:].to_broadcast([P, NB, 2, F2]), ALU.mult).then_inc(final, 1)


NE, FE = 8, 682
FC = (FE + P - 1) // P
FL = FE - (FC - 1) * P
FH = FE // 2
MT = (NT * 2 * P + NE * (P - 1)) // P
MT += MT % 2
def residual_1(nc, xs, stats, x_rows, edge_out, mix_query_t, mix_sums, w, consts):
    with Phase(nc) as ctx:
        def sb(name, shape):
            return ctx.enter_context(nc.sbuf_tensor(f"g_{name}", shape, F32))

        def ps(name, shape):
            return ctx.enter_context(nc.psum_tensor(f"g_{name}", shape, F32))

        def sem(name):
            return ctx.semaphore(f"g_{name}")

        w_o = sb("w_o", [P, 4, D])
        b_e = sb("b_e", [P, D])
        b_o = sb("b_o", [P, D])
        qt = sb("qt", [P, FOUR, 2, P])
        edge = sb("edge", [P, FOUR, D])
        den = sb("den", [P, 2, 2, 4])
        mixo = sb("mixo", [P, 2, 2, P])
        both_t = sb("both_t", [P, 2, 4, P])
        mix_p = [ps(f"mix{j}", [P, 2, D]) for j in range(2)]
        turned_p = [ps(f"turned{j}", [P, 4, P]) for j in range(2)]
        out_p = [ps(f"out{j}", [P, 512]) for j in range(2)]
        loaded, in_x = sem("loaded"), sem("in_x")
        in_q = [sem(f"in_q{i}") for i in range(FOUR)]
        in_e = [sem(f"in_e{i}") for i in range(FOUR)]
        mixed = sem("mixed")
        shared = sem("shared")
        turned = sem("turned")
        copied = sem("copied")
        mapped = sem("mapped")
        added = sem("added")
        measured = sem("measured")

        with nc.Block() as block:
            @block.sync
            def _(sp):
                sp.dma_start(w_o[:, 0:2, :], w["edge1_o"].rearrange("(c p) n -> p c n", p=P)).then_inc(loaded, 16)
                sp.dma_start(w_o[:, 2:4, :], w["mix1_o"].rearrange("(c p) n -> p c n", p=P)).then_inc(loaded, 16)
                sp.dma_start(b_e[:], rows_of(w["edge1_bo"], P)).then_inc(loaded, 16)
                sp.dma_start(b_o[:], rows_of(w["mix1_bo"], P)).then_inc(loaded, 16)

                def load(k, i):
                    t = FOUR * k + i
                    if late(k, i, FOUR, FOUR):
                        sp.wait_ge(turned, t - FOUR + 1)
                    sp.dma_start(qt[:, i, :, :].rearrange("p c n -> p (c n)"),
                                 mix_query_t[bass.ds(t, 1), :, :].rearrange("a p n -> (a p) n")).then_inc(in_q[i], 16)
                    sp.dma_start(edge[:, i, :], edge_out[bass.ds(t * P, P), :]).then_inc(in_e[i], 16)

                load(0, 0)
                load(0, 1)
                sp.dma_start(xs[:], x_rows.rearrange("(t p) d -> p t d", p=P)).then_inc(in_x, 16)
                load(0, 2)
                load(0, 3)
                with sp.Fori(1, NT // FOUR) as k:
                    for i in range(FOUR):
                        load(k, i)
                for i in range(NT % FOUR):
                    load(NT // FOUR, i)

            @block.tensor
            def _(pe):
                def mix(k, i):
                    t, b = FOUR * k + i, i % 2
                    pe.wait_ge(in_q[i], (k + 1) * 16)
                    if late(k, i, FOUR, 2):
                        pe.wait_ge(shared, 4 * (t - 1))
                    for c in range(2):
                        mm = pe.matmul(mix_p[b][:, c, 0:P + 4], qt[:, i, c, :], mix_sums[:, c, :], start=True, stop=True)
                    mm.then_inc(mixed, 1)

                def turn(k, i):
                    t, b = FOUR * k + i, i % 2
                    pe.wait_ge(in_e[i], (k + 1) * 16)
                    pe.wait_ge(shared, 4 * t + 4)
                    if late(k, i, FOUR, 2):
                        pe.wait_ge(copied, t - 1)
                    for c in range(2):
                        pe.transpose(turned_p[b][:, c, :], edge[:, i, c * P:(c + 1) * P], consts["ident"][:])
                    for c in range(2):
                        mm = pe.transpose(turned_p[b][:, 2 + c, :], mixo[:, b, c, :], consts["ident"][:])
                    mm.then_inc(turned, 1)

                def project(k, i):
                    t, b = FOUR * k + i, i % 2
                    pe.wait_ge(copied, t + 1)
                    if late(k, i, FOUR, 2):
                        pe.wait_ge(added, 2 * (t - 1))
                    for c in range(4):
                        mm = pe.matmul(out_p[b][:, 0:D], both_t[:, b, c, :], w_o[:, c, :], start=c == 0, stop=c == 3)
                    mm.then_inc(mapped, 1)

                pe.wait_ge(loaded, 64)
                pipeline(pe, [(mix, 1), (project, -1), (turn, 0)], NT, FOUR)

            @block.scalar
            def _(act):
                def copy(k, i):
                    t, b = FOUR * k + i, i % 2
                    act.wait_ge(turned, t + 1)
                    if late(k, i, FOUR, 2):
                        act.wait_ge(mapped, t - 1)
                    act.activation(both_t[:, b, :, :], turned_p[b][:, :, :], ACT.Copy).then_inc(copied, 1)

                pipeline(act, [(copy, 0)], NT, FOUR)

            @block.vector
            def _(dve):
                def divide(k, i):
                    t, b = FOUR * k + i, i % 2
                    dve.wait_ge(mixed, t + 1)
                    if late(k, i, FOUR, 2):
                        dve.wait_ge(turned, t - 1)
                    dve.tensor_scalar(den[:, b, :, :], mix_p[b][:, :, P:P + 4], 1e-6, None, ALU.add).then_inc(shared, 1)
                    dve.wait_ge(shared, 4 * t + 1)
                    dve.reciprocal(den[:, b, :, :], den[:, b, :, :]).then_inc(shared, 1)
                    dve.wait_ge(shared, 4 * t + 2)
                    for c in range(2):
                        dve.tensor_tensor(mixo[:, b, c, :].rearrange("p (h d) -> p h d", h=4),
                                          mix_p[b][:, c, 0:P].rearrange("p (h d) -> p h d", h=4),
                                          den[:, b, c, :].unsqueeze(2).to_broadcast([P, 4, F2]), ALU.mult).then_inc(shared, 1)

                def accumulate(k, i):
                    t, b = FOUR * k + i, i % 2
                    row = xs[:, bass.ds(t, 1), :].rearrange("p a d -> p (a d)")
                    dve.wait_ge(mapped, t + 1)
                    dve.tensor_tensor(row, row, out_p[b][:, 0:D], ALU.add).then_inc(added, 1)
                    dve.wait_ge(added, 2 * t + 1)
                    dve.tensor_tensor(row, row, b_o[:], ALU.add).then_inc(added, 1)
                    dve.wait_ge(added, 2 * t + 2)
                    dve.bn_stats(stats[:, bass.ds(t, 1), :].rearrange("p a d -> p (a d)"), row).then_inc(measured, 1)

                dve.wait_ge(loaded, 64)
                dve.tensor_tensor(b_o[:], b_o[:], b_e[:], ALU.add).then_inc(loaded, 1)
                dve.wait_ge(loaded, 65)
                dve.wait_ge(in_x, 16)
                pipeline(dve, [(divide, 1), (accumulate, -1)], NT, FOUR)
                dve.wait_ge(measured, NT)


def route(nc, xs, scale, shift, w, gates, slots, rows, expert_of, consts):
    with Phase(nc) as ctx:
        def sb(name, shape, dt=F32):
            return ctx.enter_context(nc.sbuf_tensor(f"r_{name}", shape, dt))

        def ps(name, shape):
            return ctx.enter_context(nc.psum_tensor(f"r_{name}", shape, F32))

        def sem(name):
            return ctx.semaphore(f"r_{name}")

        w_r = sb("w_r", [P, 2, NE])
        zeros = sb("zeros", [P, D])
        xn = sb("xn", [P, 2, D])
        xt = sb("xt", [P, 2, 2, P])
        prob = sb("prob", [P, NT, NE])
        rest = sb("rest", [P, NT, NE])
        rank_of = sb("rank_of", [P, NT, NE])
        found = sb("found", [P, NT, NE])
        hot = [sb(f"hot{c}", [P, NT, NE]) for c in range(2)]
        hot_b = sb("hot_b", [P, NT, NE], BF16)
        top = [sb(f"top{c}", [P, NT]) for c in range(2)]
        place = sb("place", [P, NT])
        slot = sb("slot", [P, NT, NE])
        total = sb("total", [P, NT, NE])
        upto = sb("upto", [P, NT, NE])
        ones_row = sb("ones_row", [P, NT])
        slot_f = sb("slot_f", [P, NT, 2])
        tiles_i = sb("tiles_i", [P, NE], I32)
        tiles = sb("tiles", [P, NE])
        ends = sb("ends", [P, NE])
        start = sb("start", [P, NE])
        before = sb("before", [P, NE])
        expert = sb("expert", [P, 1])
        expert_i = sb("expert_i", [P, 1], I32)
        turned_p = [ps(f"turned{j}", [P, 2, P]) for j in range(2)]
        logit_p = ps("logit", [P, 512])
        rank_p = ps("rank", [P, 512])
        total_p = ps("total_p", [P, 512])
        loaded = sem("loaded")
        normed, turned, copied = sem("normed"), sem("turned"), sem("copied")
        scored = sem("scored")
        exped = sem("exped")
        steps = sem("steps")
        counted = sem("counted")
        mapped = sem("mapped")
        cleared = sem("cleared")
        COLS = NT * NE

        def flat(ap):
            return ap.rearrange("p t e -> p (t e)")

        with nc.Block() as block:
            @block.sync
            def _(sp):
                with nc.allow_non_contiguous_dma(reason="eight columns"):
                    sp.dma_start(w_r[:], w["moe_router_t"].rearrange("(c p) n -> p c n", p=P)).then_inc(loaded, 16)
                sp.wait_ge(cleared, 1)
                sp.dma_start(rows.rearrange("(t p) d -> p t d", p=P),
                             zeros[:].unsqueeze(1).to_broadcast([P, MT, D])).then_inc(cleared, 16)
                sp.wait_ge(mapped, 1)
                with nc.allow_non_contiguous_dma(reason="128 words"):
                    sp.dma_start(expert_of.unsqueeze(1), expert_i[:]).then_inc(mapped, 16)
                sp.wait_ge(mapped, 17)
                sp.wait_ge(cleared, 17)

            @block.gpsimd
            def _(pool):
                pool.memset(zeros[:], 0.0).then_inc(cleared, 1)
                pool.iota(rank_of[:], pattern=[[0, NT], [-1, NE]], base=NE, channel_multiplier=0,
                          allow_small_or_imprecise_dtypes=True).then_inc(loaded, 1)

            @block.scalar
            def _(act):
                def norm(k, j):
                    t = 2 * k + j
                    if second(k, j):
                        act.wait_ge(turned, t - 1)
                    act.activation(xn[:, j, :], xs[:, bass.ds(t, 1), :].rearrange("p a d -> p (a d)"), ACT.Identity,
                                   bias=shift[:, bass.ds(t, 1)], scale=scale[:, bass.ds(t, 1)]).then_inc(normed, 1)

                norm(0, 0)
                norm(0, 1)
                over_tiles(act, 1, norm)
                act.wait_ge(steps, 3)
                act.activation(flat(prob[:]), flat(rest[:]), ACT.Exp).then_inc(exped, 1)

            @block.tensor
            def _(pe):
                def turn(k, i):
                    t, b = FOUR * k + i, i % 2
                    pe.wait_ge(normed, t + 1)
                    if late(k, i, FOUR, 2):
                        pe.wait_ge(copied, t - 1)
                    for c in range(2):
                        mm = pe.transpose(turned_p[b][:, c, :], xn[:, b, c * P:(c + 1) * P], consts["ident"][:])
                    mm.then_inc(turned, 1)

                def score(k, i):
                    t, b = FOUR * k + i, i % 2
                    pe.wait_ge(copied, t + 1)
                    for c in range(2):
                        mm = pe.matmul(logit_p[:, bass.ds(t * NE, NE)], xt[:, b, c, :], w_r[:, c, :],
                                       start=c == 0, stop=c == 1)
                    mm.then_inc(scored, 1)

                pe.wait_ge(loaded, 17)
                pipeline(pe, [(turn, 1), (score, 0)], NT, FOUR)
                pe.wait_ge(steps, 18)
                pe.matmul(rank_p[:, 0:COLS], consts["tri"][:], flat(hot_b[:]), start=True, stop=True).then_inc(counted, 1)
                pe.matmul(total_p[:, 0:COLS], consts["ones"][:], flat(hot_b[:]), start=True, stop=True).then_inc(counted, 1)

            @block.vector
            def _(dve):
                def copy(k, i):
                    t, b = FOUR * k + i, i % 2
                    dve.wait_ge(turned, t + 1)
                    if late(k, i, FOUR, 2):
                        dve.wait_ge(scored, t - 1)
                    dve.tensor_copy(xt[:, b, :, :], turned_p[b][:, :, :]).then_inc(copied, 1)

                pipeline(dve, [(copy, 0)], NT, FOUR)
                count = [0]

                def done(op):
                    count[0] += 1
                    op.then_inc(steps, 1)
                    dve.wait_ge(steps, count[0])

                def wide(ap):
                    return ap.unsqueeze(2).to_broadcast([P, NT, NE])

                dve.wait_ge(loaded, 17)
                dve.wait_ge(scored, NT)
                logits = logit_p[:, 0:COLS].rearrange("p (t e) -> p t e", e=NE)
                done(dve.memset(ones_row[:], 1.0))
                done(dve.tensor_reduce(place[:], logits, AX.X, ALU.max))
                done(dve.tensor_tensor(rest[:], logits, wide(place[:]), ALU.subtract))
                dve.wait_ge(exped, 1)
                done(dve.tensor_reduce(place[:], prob[:], AX.X, ALU.add))
                done(dve.reciprocal(place[:], place[:]))
                done(dve.tensor_tensor(prob[:], prob[:], wide(place[:]), ALU.mult))
                for c in range(2):
                    of = (prob, rest)[c]
                    done(dve.tensor_reduce(top[c][:], of[:], AX.X, ALU.max))
                    done(dve.tensor_tensor(found[:], of[:], wide(top[c][:]), ALU.is_equal))
                    done(dve.tensor_tensor(found[:], found[:], rank_of[:], ALU.mult))
                    done(dve.tensor_reduce(place[:], found[:], AX.X, ALU.max))
                    done(dve.tensor_tensor(hot[c][:], found[:], wide(place[:]), ALU.is_equal))
                    if c == 0:
                        done(dve.scalar_tensor_tensor(rest[:], hot[0][:], -2.0, prob[:], ALU.mult, ALU.add))
                done(dve.tensor_tensor(hot_b[:], hot[0][:], hot[1][:], ALU.add))
                done(dve.tensor_tensor(place[:], top[0][:], top[1][:], ALU.add))
                done(dve.tensor_scalar(place[:], place[:], 1e-9, None, ALU.add))
                done(dve.reciprocal(place[:], place[:]))
                for c in range(2):
                    done(dve.tensor_tensor(gates[:, :, c], top[c][:], place[:], ALU.mult))
                dve.wait_ge(counted, 2)
                done(dve.tensor_copy(flat(total[:]), total_p[:, 0:COLS]))
                for e in range(NE):
                    op = dve.tensor_tensor_scan(upto[:, :, e], ones_row[:], total[:, :, e], 0.0, ALU.mult, ALU.add)
                    done(op)
                done(dve.tensor_tensor(slot[:], upto[:], total[:], ALU.subtract))
                done(dve.tensor_tensor(flat(slot[:]), flat(slot[:]), rank_p[:, 0:COLS], ALU.add))
                done(dve.tensor_scalar(tiles_i[:], upto[:, NT - 1, :], float(P - 1), None, ALU.add))
                done(dve.tensor_scalar(tiles_i[:], tiles_i[:], 7, None, ALU.arith_shift_right))
                done(dve.tensor_copy(tiles[:], tiles_i[:]))
                done(dve.tensor_tensor_scan(ends[:], ones_row[:, 0:NE], tiles[:], 0.0, ALU.mult, ALU.add))
                done(dve.tensor_tensor(start[:], ends[:], tiles[:], ALU.subtract))
                done(dve.tensor_scalar(start[:], start[:], float(P), None, ALU.mult))
                done(dve.tensor_tensor(slot[:], slot[:], start[:].unsqueeze(1).to_broadcast([P, NT, NE]), ALU.add))
                for c in range(2):
                    done(dve.tensor_tensor(found[:], slot[:], hot[c][:], ALU.mult))
                    done(dve.tensor_reduce(slot_f[:, :, c], found[:], AX.X, ALU.add))
                done(dve.tensor_copy(slots[:], slot_f[:]))
                done(dve.tensor_scalar(before[:], ends[:], consts["tile_no"][:, 0:1], None, ALU.is_le, ALU.add,
                                       accum_out=expert[:]))
                done(dve.tensor_scalar(expert[:], expert[:], float(NE - 1), None, ALU.min))
                op = dve.tensor_copy(expert_i[:], expert[:])
                op.then_inc(mapped, 1)


def dispatch(nc, xs, scale, shift, slots, rows, w, w1, w3, w2, consts):
    with Phase(nc) as ctx:
        stage = [ctx.enter_context(nc.sbuf_tensor(f"d_stage{i}", [P, D], F32)) for i in range(FOUR)]
        index = [ctx.enter_context(nc.sbuf_tensor(f"d_index{i}", [P, 2], I32)) for i in range(FOUR)]
        loaded = ctx.semaphore("d_loaded")
        staged = ctx.semaphore("d_staged")
        indexed = ctx.semaphore("d_indexed")
        taken = ctx.semaphore("d_taken")
        put = row_moves(consts, FOUR)
        with nc.Block() as block:
            @block.sync
            def _(sp):
                for c in range(2):
                    sp.dma_start(w1[:, c, :, :], w["moe_w1_t"][c * P:(c + 1) * P, :, :]).then_inc(loaded, 16)
                    sp.dma_start(w3[:, c, :, :], w["moe_w3_t"][c * P:(c + 1) * P, :, :]).then_inc(loaded, 16)
                for f in range(FC):
                    n = FL if f == FC - 1 else P
                    sp.dma_start(w2[0:n, f, :, :], w["moe_w2_t"][f * P:f * P + n, :, :]).then_inc(loaded, 16)
                sp.wait_ge(loaded, 16 * (4 + FC))

            @block.scalar
            def _(act):
                def norm(k, i):
                    t = FOUR * k + i
                    if late(k, i, FOUR, FOUR):
                        act.wait_ge(put[i], k * 32)
                    act.activation(stage[i][:], xs[:, bass.ds(t, 1), :].rearrange("p a d -> p (a d)"), ACT.Identity,
                                   bias=shift[:, bass.ds(t, 1)], scale=scale[:, bass.ds(t, 1)]).then_inc(staged, 1)

                pipeline(act, [(norm, 0)], NT, FOUR)

            @block.gpsimd
            def _(pool):
                def scatter(k, i):
                    t = FOUR * k + i
                    if late(k, i, FOUR, FOUR):
                        pool.wait_ge(put[i], k * 32)
                    pool.tensor_copy(index[i][:], slots[:, bass.ds(t, 1), :].rearrange("p a c -> p (a c)")).then_inc(indexed, 1)
                    pool.wait_ge(indexed, t + 1)
                    pool.wait_ge(staged, t + 1)
                    pool.sem_inc(taken, 1)
                    for c in range(2):
                        pool.indirect_dma_start(
                            out=rows, out_offset=bass.IndirectOffsetOnAxis(ap=index[i][:, c:c + 1], axis=0),
                            in_=stage[i][:], in_offset=None).then_inc(put[i], 16)

                pipeline(pool, [(scatter, 0)], NT, FOUR)
                for i in range(FOUR):
                    pool.wait_ge(put[i], 32 * len(range(i, NT, FOUR)))


def experts(nc, rows, products, expert_of, w1, w3, w2, consts):
    with Phase(nc) as ctx:
        def sb(name, shape, dt=F32):
            return ctx.enter_context(nc.sbuf_tensor(f"m_{name}", shape, dt))

        def ps(name, shape):
            return ctx.enter_context(nc.psum_tensor(f"m_{name}", shape, F32))

        def sem(name):
            return ctx.semaphore(f"m_{name}")

        expert = sb("expert", [1, P], I32)
        row = sb("row", [P, 2, D])
        xt = sb("xt", [P, 2, 2, P])
        gate = sb("gate", [P, 2, FH])
        hidden = sb("hidden", [P, FE])
        hidden_t = sb("hidden_t", [P, FC, P])
        out = sb("out", [P, 2, D])
        h1_p = ps("h1", [P, 2, 512])
        h3_p = ps("h3", [P, 2, 512])
        turned_p = ps("turned", [P, 2, P])
        flip_p = ps("flip", [P, 8, P])
        out_p = ps("out_p", [P, 512])

        loaded = sem("loaded")
        in_row = [sem(f"in_row{j}") for j in range(2)]
        turned, copied = sem("turned"), sem("copied")
        first, third = sem("first"), sem("third")
        gated = sem("gated")
        hid = sem("hid")
        flipped, flipped_sb = sem("flipped"), sem("flipped_sb")
        second_ = sem("second")
        evacuated = sem("evacuated")
        out_done = [sem(f"out_done{j}") for j in range(2)]

        with nc.Block() as block:
            @block.sync
            def _(sp):
                sp.dma_start(expert[:], expert_of.unsqueeze(0)).then_inc(loaded, 16)

                def load(k, j):
                    t = 2 * k + j
                    if late(k, j, 2, 2):
                        sp.wait_ge(turned, t - 1)
                    sp.dma_start(row[:, j, :], rows[bass.ds(t * P, P), :]).then_inc(in_row[j], 16)

                def store(k, j):
                    t = 2 * k + j
                    sp.wait_ge(evacuated, t + 1)
                    sp.dma_start(products[bass.ds(t * P, P), :], out[:, j, :]).then_inc(out_done[j], 16)

                pipeline(sp, [(load, 2), (store, -1)], MT, 2)
                for j in range(2):
                    sp.wait_ge(out_done[j], 16 * (MT // 2))

            @block.tensor
            def _(pe):
                def turn(k, j):
                    t = 2 * k + j
                    pe.wait_ge(in_row[j], (k + 1) * 16)
                    if late(k, j, 2, 1):
                        pe.wait_ge(copied, t)
                    for c in range(2):
                        mm = pe.transpose(turned_p[:, c, :], row[:, j, c * P:(c + 1) * P], consts["ident"][:])
                    mm.then_inc(turned, 1)

                def expand(k, j):
                    t = 2 * k + j
                    e = pe.value_load(expert[0:1, bass.ds(t, 1)], min_val=0, max_val=NE - 1)
                    pe.wait_ge(copied, t + 1)
                    if late(k, j, 2, 1):
                        pe.wait_ge(hid, 2 * t)
                    for weight, into, done in ((w1, h1_p, first), (w3, h3_p, third)):
                        for half in range(2):
                            for c in range(2):
                                mm = pe.matmul(into[:, half, 0:FH], xt[:, j, c, :],
                                               weight[:, c, bass.ds(e, 1), half * FH:(half + 1) * FH].rearrange("p a n -> p (a n)"),
                                               start=c == 0, stop=c == 1)
                        mm.then_inc(done, 1)

                def flip(k, j):
                    t = 2 * k + j
                    pe.wait_ge(hid, 2 * t + 2)
                    if late(k, j, 2, 1):
                        pe.wait_ge(flipped_sb, t)
                    for f in range(FC):
                        n = FL if f == FC - 1 else P
                        mm = pe.transpose(flip_p[0:n, f, :], hidden[:, f * P:f * P + n], consts["ident"][:])
                    mm.then_inc(flipped, 1)

                def contract(k, j):
                    t = 2 * k + j
                    e = pe.value_load(expert[0:1, bass.ds(t, 1)], min_val=0, max_val=NE - 1)
                    pe.wait_ge(flipped_sb, t + 1)
                    if late(k, j, 2, 1):
                        pe.wait_ge(evacuated, t)
                    for f in range(FC):
                        n = FL if f == FC - 1 else P
                        mm = pe.matmul(out_p[:, 0:D], hidden_t[0:n, f, :],
                                       w2[0:n, f, bass.ds(e, 1), :].rearrange("p a n -> p (a n)"),
                                       start=f == 0, stop=f == FC - 1)
                    mm.then_inc(second_, 1)

                pe.wait_ge(loaded, 16)
                pipeline(pe, [(expand, 0), (turn, 1), (contract, -1), (flip, 0)], MT, 2)

            @block.scalar
            def _(act):
                def copy_rows(k, j):
                    t = 2 * k + j
                    act.wait_ge(turned, t + 1)
                    if late(k, j, 2, 2):
                        act.wait_ge(third, t - 1)
                    act.activation(xt[:, j, :, :], turned_p[:, :, :], ACT.Copy).then_inc(copied, 1)

                def sigmoid(k, j):
                    t = 2 * k + j
                    act.wait_ge(first, t + 1)
                    if late(k, j, 2, 1):
                        act.wait_ge(hid, 2 * t - 1)
                    act.activation(gate[:], h1_p[:, :, 0:FH], ACT.Sigmoid).then_inc(gated, 1)

                def copy_hidden(k, j):
                    t = 2 * k + j
                    act.wait_ge(flipped, t + 1)
                    if late(k, j, 2, 1):
                        act.wait_ge(second_, t)
                    act.activation(hidden_t[:, 0:FC - 1, :], flip_p[:, 0:FC - 1, :], ACT.Copy)
                    act.activation(hidden_t[0:FL, FC - 1, :], flip_p[0:FL, FC - 1, :], ACT.Copy).then_inc(flipped_sb, 1)

                pipeline(act, [(sigmoid, 0), (copy_rows, 1), (copy_hidden, 0)], MT, 2)

            @block.vector
            def _(dve):
                def halves(ap):
                    return ap.rearrange("p (a n) -> p a n", a=2)

                def hide(k, j):
                    t = 2 * k + j
                    dve.wait_ge(gated, t + 1)
                    if late(k, j, 2, 1):
                        dve.wait_ge(flipped, t)
                    dve.tensor_tensor(halves(hidden[:]), gate[:], h1_p[:, :, 0:FH], ALU.mult).then_inc(hid, 1)
                    dve.wait_ge(hid, 2 * t + 1)
                    dve.wait_ge(third, t + 1)
                    dve.tensor_tensor(halves(hidden[:]), halves(hidden[:]), h3_p[:, :, 0:FH], ALU.mult).then_inc(hid, 1)

                def evacuate(k, j):
                    t = 2 * k + j
                    dve.wait_ge(second_, t + 1)
                    if late(k, j, 2, 2):
                        dve.wait_ge(out_done[j], k * 16)
                    dve.tensor_copy(out[:, j, :], out_p[:, 0:D]).then_inc(evacuated, 1)

                pipeline(dve, [(hide, 0), (evacuate, -1)], MT, 2)


def combine(nc, xs, gates, slots, products, y, consts):
    with Phase(nc) as ctx:
        got = ctx.enter_context(nc.sbuf_tensor("k_got", [P, FOUR, 2, D], F32))
        index = [ctx.enter_context(nc.sbuf_tensor(f"k_index{i}", [P, 2], I32)) for i in range(FOUR)]
        indexed = ctx.semaphore("k_indexed")
        taken = ctx.semaphore("k_taken")
        added = ctx.semaphore("k_added")
        stored = ctx.semaphore("k_stored")
        gathered = row_moves(consts, FOUR)
        with nc.Block() as block:
            @block.gpsimd
            def _(pool):
                def gather(k, i):
                    t = FOUR * k + i
                    if late(k, i, FOUR, FOUR):
                        pool.wait_ge(gathered[i], k * 32)
                    pool.tensor_copy(index[i][:], slots[:, bass.ds(t, 1), :].rearrange("p a c -> p (a c)")).then_inc(indexed, 1)
                    pool.wait_ge(indexed, t + 1)
                    if late(k, i, FOUR, FOUR):
                        pool.wait_ge(added, 2 * (t - FOUR + 1))
                    pool.sem_inc(taken, 1)
                    for c in range(2):
                        pool.indirect_dma_start(
                            out=got[:, i, c, :], out_offset=None, in_=products,
                            in_offset=bass.IndirectOffsetOnAxis(ap=index[i][:, c:c + 1], axis=0)).then_inc(gathered[i], 16)

                pipeline(pool, [(gather, 0)], NT, FOUR)

            @block.vector
            def _(dve):
                def add(k, i):
                    t = FOUR * k + i
                    x = xs[:, bass.ds(t, 1), :].rearrange("p a d -> p (a d)")
                    dve.wait_ge(gathered[i], (k + 1) * 32)
                    for c in range(2):
                        if c:
                            dve.wait_ge(added, 2 * t + 1)
                        dve.scalar_tensor_tensor(x, got[:, i, c, :],
                                                 gates[:, bass.ds(t, 1), c:c + 1].rearrange("p a c -> p (a c)"), x,
                                                 ALU.mult, ALU.add).then_inc(added, 1)

                pipeline(dve, [(add, 0)], NT, FOUR)

            @block.sync
            def _(sp):
                def store(k, i):
                    t = FOUR * k + i
                    sp.wait_ge(added, 2 * t + 2)
                    sp.dma_start(y[bass.ds(t * P, P), :],
                                 xs[:, bass.ds(t, 1), :].rearrange("p a d -> p (a d)")).then_inc(stored, 16)

                pipeline(sp, [(store, 0)], NT - 1, FOUR)
                sp.wait_ge(added, 2 * NT)
                sp.dma_start(y[(NT - 1) * P:N, :], xs[0:LAST, NT - 1, :]).then_inc(stored, 16)
                sp.wait_ge(stored, 16 * NT)


def graph_transformer(nc, args, y):
    w = args

    def dram(name, shape, dt=F32):
        return nc.dram_tensor(name, shape, dt).ap()

    recs = [dram(f"recs{i}", (P * SORT_TILES, REC)) for i in range(2)]
    tile_bucket = [dram(f"tile_bucket{i}", (8 * P,), I32) for i in range(2)]
    table_0, edge_0 = dram("table_0", (NP, TAB0)), dram("edge_0", (NP, D))
    table_1, edge_1 = dram("table_1", (NP, TAB1)), dram("edge_1", (NP, D))
    xn_t = dram("xn_t", (NT, P, D))
    weights = dram("slice_weights", (NP, HG))
    x_rows = dram("x_rows", (NP, D))
    query_t, mix_query_t = dram("query_t", (NB + 8, P, 2 * BN)), dram("mix_query_t", (NT, P, D))
    rows, products = dram("rows", (MT * P, D)), dram("products", (MT * P, D))
    expert_of = dram("expert_of", (P,), I32)

    with ExitStack() as whole:
        def keep(ctx, name, shape, dt=F32):
            return ctx.enter_context(nc.sbuf_tensor(name, shape, dt))

        consts = make_constants(nc, whole)
        stats = keep(whole, "stats", [P, NT, 6])
        scale, shift = keep(whole, "scale", [P, NT]), keep(whole, "shift", [P, NT])
        mix_sums = keep(whole, "mix_sums", [P, 2, P + 4])
        with ExitStack() as ctx:
            xs = keep(ctx, "xs", [P, NT, D])
            with ExitStack() as inner:
                mix, mix_bias = keep(inner, "mix", [P, 2, D]), keep(inner, "mix_bias", [P, D])
                first_stats(nc, args["x"], xs, stats)
                normal_factors(nc, "norm0", stats, scale, shift)
                sort_edges(nc, "sort0", args["dst_key"], args["src_other"], args["attr"], recs[0], tile_bucket[0], consts)
                node_pass_0(nc, xs, scale, shift, w, table_0, xn_t, mix, mix_bias, consts)
                edge_attention_0(nc, recs[0], tile_bucket[0], table_0, edge_0, consts)
                residual_0(nc, xs, stats, xn_t, edge_0, mix, mix_bias)
            normal_factors(nc, "norm1", stats, scale, shift)
            with ExitStack() as inner:
                tokens, out_map = keep(inner, "tokens", [P, 4, D + 1]), keep(inner, "out_map", [P, 4, D])
                slice_weights(nc, xs, scale, shift, w, weights, tokens, consts)
                slice_attention(nc, w, tokens, out_map, consts)
                residual_slices(nc, xs, stats, weights, out_map, w["ffn0_bout"], x_rows, consts)
            normal_factors(nc, "norm2", stats, scale, shift)
            sort_edges(nc, "sort1", args["src_key"], args["dst_other"], None, recs[1], tile_bucket[1], consts)
            node_pass_1(nc, xs, scale, shift, w, table_1, query_t, mix_query_t, mix_sums, consts)
        edge_attention_1(nc, recs[1], tile_bucket[1], table_1, query_t, edge_1, consts)
        xs = keep(whole, "xs_1", [P, NT, D])
        gates, slots = keep(whole, "gates", [P, NT, 2]), keep(whole, "slots", [P, NT, 2], I32)
        residual_1(nc, xs, stats, x_rows, edge_1, mix_query_t, mix_sums, w, consts)
        normal_factors(nc, "norm3", stats, scale, shift)
        route(nc, xs, scale, shift, w, gates, slots, rows, expert_of, consts)
        w1, w3 = keep(whole, "w1", [P, 2, NE, FE]), keep(whole, "w3", [P, 2, NE, FE])
        w2 = keep(whole, "w2", [P, FC, NE, D])
        dispatch(nc, xs, scale, shift, slots, rows, w, w1, w3, w2, consts)
        experts(nc, rows, products, expert_of, w1, w3, w2, consts)
        combine(nc, xs, gates, slots, products, y, consts)


def laid_out(inputs):
    a = {k: np.asarray(v) for k, v in inputs.items()}
    x = np.zeros((NP, D), a["x"].dtype)
    x[:N] = a["x"]

    def edges(values, pad):
        out = np.full((EP,) + values.shape[1:], pad, values.dtype)
        out[:E] = values
        return out.reshape((IN_TILES, P) + values.shape[1:]).swapaxes(0, 1)

    by_head = np.arange(D).reshape(F2, H2).T.reshape(-1)
    gnn1, mix1, moe = (lambda n: a["L1_gnn_" + n]), (lambda n: a["L1_mix_" + n]), (lambda n: a["L1_ffn_" + n])
    gnn0, mix0, ffn0 = (lambda n: a["L0_gnn_" + n]), (lambda n: a["L0_mix_" + n]), (lambda n: a["L0_ffn_" + n])
    out = {
        "x": x,
        "dst_key": edges(a["dst"], PAD_KEY), "dst_other": edges(a["dst"], 0),
        "src_key": edges(a["src"], PAD_KEY), "src_other": edges(a["src"], 0),
        "attr": edges(a["edge_attr_2"], 0),
        "edge_f_t": gnn0("W_forward").T, "edge_r_t": gnn0("W_reverse").T,
        "edge_f": gnn0("W_forward"), "edge_r": gnn0("W_reverse"), "edge_heads_t": gnn0("attn_forward")[0].T,
        "mix0_k_t": mix0("Wk").T, "mix0_v_t": mix0("Wv").T, "mix0_bk": mix0("bk"), "mix0_bv": mix0("bv"),
        "mix0_q": mix0("Wq"), "mix0_bq": mix0("bq"), "mix0_fc_t": mix0("Wfc").T, "mix0_bfc": mix0("bfc"),
        "ffn0_x_t": ffn0("W_x").T, "ffn0_slice": ffn0("W_slice"), "ffn0_bx": ffn0("b_x"),
        "ffn0_bslice": ffn0("b_slice"), "ffn0_temp": ffn0("temperature").reshape(H1),
        "ffn0_fx": ffn0("W_fx"), "ffn0_bfx": ffn0("b_fx"), "ffn0_out": ffn0("W_out"), "ffn0_bout": ffn0("b_out"),
        "ffn0_q": ffn0("W_q"), "ffn0_k": ffn0("W_k"), "ffn0_v": ffn0("W_v"),
        "edge1_q": gnn1("Wq")[:, by_head], "edge1_k": gnn1("Wk")[:, by_head], "edge1_v": gnn1("Wv")[:, by_head],
        "edge1_bq": gnn1("bq")[by_head], "edge1_bk": gnn1("bk")[by_head], "edge1_bv": gnn1("bv")[by_head],
        "edge1_o": gnn1("Wo")[by_head], "edge1_bo": gnn1("bo"),
        "mix1_q": mix1("wq"), "mix1_k": mix1("wk"), "mix1_v": mix1("wv"), "mix1_o": mix1("wo"),
        "mix1_bq": mix1("bq"), "mix1_bk": mix1("bk"), "mix1_bv": mix1("bv"), "mix1_bo": mix1("bo"),
        "moe_router_t": moe("router_w").T, "moe_w1_t": moe("w1").transpose(2, 0, 1),
        "moe_w3_t": moe("w3").transpose(2, 0, 1), "moe_w2_t": moe("w2").transpose(2, 0, 1),
    }
    return {k: np.ascontiguousarray(v) for k, v in out.items()}


def kernel(**inputs):
    import concourse.bacc as bacc
    from concourse.bass_utils import run_bass_kernel_spmd

    arrays = laid_out(inputs)
    nc = bacc.Bacc("TRN2", target_bir_lowering=False, num_devices=1)
    args = {k: nc.dram_tensor(f"in_{k}_dram", v.shape, mybir.dt.from_np(v.dtype), kind="ExternalInput").ap()
            for k, v in arrays.items()}
    y = nc.dram_tensor("out_0_dram", (N, D), F32, kind="ExternalOutput").ap()
    graph_transformer(nc, args, y)
    result = run_bass_kernel_spmd(nc, [{f"in_{k}_dram": v for k, v in arrays.items()}], core_ids=[0])
    return result.results[0]["out_0_dram"]
```
